# Optimizing a Trainium2 kernel written in Bass

```python
import numpy as np
import jax
import jax.numpy as jnp

def _softmax(x, axis=-1):
    return jax.nn.softmax(x, axis=axis)

def _gelu(x):
    return jax.nn.gelu(x, approximate=True)

def _silu(x):
    return jax.nn.silu(x)

def _sigmoid(x):
    return jax.nn.sigmoid(x)

def _layernorm(x, axis=-1, eps=1e-05):
    m = jnp.mean(x, axis=axis, keepdims=True)
    v = jnp.var(x, axis=axis, keepdims=True)
    return (x - m) / jnp.sqrt(v + eps)

def _scatter_add(tgt, idx, src, axis=0):
    return tgt.at[idx].add(src)

def _segment_sum(src, seg, n):
    return jax.ops.segment_sum(src, seg, n)
kernel_name = 'mk_flamingo_gated_d1_seqx_r4_69797d'

def setup_inputs(seed: int=0):
    np.random.seed(seed)
    _w = jnp.asarray

    def _rec_inputs():
        import jax
        import jax.numpy as jnp
        _rk = jax.random.key(seed)
        x = 7.22e-05 + 1 * jax.random.normal(jax.random.fold_in(_rk, 1), (1, 2048, 256), jnp.float32)
        _lenS = 2048 - jax.random.randint(jax.random.fold_in(_rk, 7), (1,), 0, max(1, 2048 // 4) + 1, jnp.int32)
        _lenS2 = 1601 - jax.random.randint(jax.random.fold_in(_rk, 8), (1,), 0, max(1, 1601 // 4) + 1, jnp.int32)
        _ctx_1024P = jax.random.normal(jax.random.fold_in(_rk, 11), (1, 16, 256), jnp.float32)
        _ctx_1024c = jax.random.dirichlet(jax.random.fold_in(_rk, 511), 0.3 * jnp.ones((16,), jnp.float32), (1, 1601))
        _ctx_1024t = jnp.einsum('bsk,bkd->bsd', _ctx_1024c, _ctx_1024P)
        _ctx_1024t = _ctx_1024t * jax.lax.rsqrt(jnp.mean(jnp.square(_ctx_1024t)) + 1e-12) * 0.953939
        ctx_1024 = 4.13588e-05 + 0.999923 * (_ctx_1024t + 0.3 * jax.random.normal(jax.random.fold_in(_rk, 611), (1, 1601, 256), jnp.float32))
        _g = jax.random.normal(jax.random.fold_in(_rk, 9001), (2, 1), jnp.float32)
        _g = jnp.sign(_g) * jnp.maximum(jnp.abs(_g), 1.0) + (_g == 0) * 1.0
        g_xattn = _g[0]
        g_ffn = _g[1]
        return (x, ctx_1024, g_xattn, g_ffn)
    x, ctx_1024, g_xattn, g_ffn = _rec_inputs()

    def _L0_xattn_setup():
        import jax, jax.numpy as jnp
        import numpy as np
        KDIM = 64
        key = jax.random.key(seed)
        ks = jax.random.split(key, 7)
        B, S, M, H, D = (4, 512, 256, 16, 64)
        q = jax.random.normal(ks[0], (B, S, M), dtype=jnp.float32)
        k = jax.random.normal(ks[1], (B, S, M), dtype=jnp.float32)
        v = jax.random.normal(ks[2], (B, S, M), dtype=jnp.float32)
        sc = 1.0 / np.sqrt(M)
        Wq = jax.random.normal(ks[3], (H, M, D), dtype=jnp.float32) * sc
        Wk = jax.random.normal(ks[4], (H, M, D), dtype=jnp.float32) * sc
        Wv = jax.random.normal(ks[5], (H, M, D), dtype=jnp.float32) * sc
        Wo = jax.random.normal(ks[6], (H * D, M), dtype=jnp.float32) * (1.0 / np.sqrt(H * D))
        return {'q': q, 'k': k, 'v': v, 'Wq': Wq, 'Wk': Wk, 'Wv': Wv, 'Wo': Wo}
    _L0_xattn_all = _L0_xattn_setup()
    _L0_xattn_in = {k: v for k, v in _L0_xattn_all.items() if k in ('Wq', 'Wk', 'Wv', 'Wo')}
    del _L0_xattn_all

    def _L0_ffn_setup():
        import jax, jax.numpy as jnp
        import numpy as np
        BLOCK = 32
        W_BITS = 4
        ACT_BITS = 16

        def act_qdq(x):
            qmax = 2.0 ** (ACT_BITS - 1) - 1.0
            scale = jnp.maximum(jnp.max(jnp.abs(x)) / qmax, 1e-12)
            return jnp.clip(jnp.round(x / scale), -qmax - 1.0, qmax) * scale

        def fixed_qdq_u16(x):
            scale = 1.0 / 65536.0
            return jnp.clip(jnp.round(x / scale), 0.0, 65535.0) * scale

        def lpbq_dequant(w):
            O, I = w.shape
            qmax = 2.0 ** (W_BITS - 1) - 1.0
            wb = w.reshape(O, I // BLOCK, BLOCK)
            s = jnp.maximum(jnp.max(jnp.abs(wb), axis=-1, keepdims=True) / qmax, 1e-12)
            wq = jnp.clip(jnp.round(wb / s), -qmax - 1.0, qmax) * s
            return wq.reshape(O, I)
        key = jax.random.key(seed)
        k1, k2, k3, k4 = jax.random.split(key, 4)
        B, S, H, I = (2, 1024, 256, 768)
        x = jax.random.normal(k1, (B, S, H), jnp.float32)
        w_gate = jax.random.normal(k2, (I, H), jnp.float32) * 0.02
        w_up = jax.random.normal(k3, (I, H), jnp.float32) * 0.02
        w_down = jax.random.normal(k4, (H, I), jnp.float32) * 0.02
        return {'x': x, 'w_gate': w_gate, 'w_up': w_up, 'w_down': w_down}
    _L0_ffn_all = _L0_ffn_setup()
    _L0_ffn_in = {k: v for k, v in _L0_ffn_all.items() if k in ('w_gate', 'w_up', 'w_down')}
    del _L0_ffn_all
    return {'x': x, 'ctx_1024': ctx_1024, 'g_xattn': g_xattn, 'g_ffn': g_ffn, 'L0_xattn_Wq': _L0_xattn_in['Wq'], 'L0_xattn_Wk': _L0_xattn_in['Wk'], 'L0_xattn_Wv': _L0_xattn_in['Wv'], 'L0_xattn_Wo': _L0_xattn_in['Wo'], 'L0_ffn_w_gate': _L0_ffn_in['w_gate'], 'L0_ffn_w_up': _L0_ffn_in['w_up'], 'L0_ffn_w_down': _L0_ffn_in['w_down']}

def reference(x, ctx_1024, g_xattn, g_ffn, L0_xattn_Wq, L0_xattn_Wk, L0_xattn_Wv, L0_xattn_Wo, L0_ffn_w_gate, L0_ffn_w_up, L0_ffn_w_down):
    import jax
    import jax.numpy as jnp

    def _L0_xattn_ref(q, k, v, Wq, Wk, Wv, Wo):
        import jax, jax.numpy as jnp
        import numpy as np
        KDIM = 64
        Q = jnp.einsum('bsm,hmd->bhsd', q, Wq)
        K = jnp.einsum('bsm,hmd->bhsd', k, Wk)
        V = jnp.einsum('bsm,hmd->bhsd', v, Wv)
        scores = jnp.einsum('bhsd,bhtd->bhst', Q, K) / jnp.sqrt(jnp.asarray(KDIM, Q.dtype))
        A = jax.nn.softmax(scores, axis=-1)
        O = jnp.einsum('bhst,bhtd->bhsd', A, V)
        B, H, S, D = O.shape
        Ocat = jnp.transpose(O, (0, 2, 1, 3)).reshape(B, S, H * D)
        return Ocat @ Wo

    def _L0_ffn_ref(x, w_gate, w_up, w_down):
        import jax, jax.numpy as jnp
        import numpy as np
        BLOCK = 32
        W_BITS = 4
        ACT_BITS = 16

        def act_qdq(x):
            qmax = 2.0 ** (ACT_BITS - 1) - 1.0
            scale = jnp.maximum(jnp.max(jnp.abs(x)) / qmax, 1e-12)
            return jnp.clip(jnp.round(x / scale), -qmax - 1.0, qmax) * scale

        def fixed_qdq_u16(x):
            scale = 1.0 / 65536.0
            return jnp.clip(jnp.round(x / scale), 0.0, 65535.0) * scale

        def lpbq_dequant(w):
            O, I = w.shape
            qmax = 2.0 ** (W_BITS - 1) - 1.0
            wb = w.reshape(O, I // BLOCK, BLOCK)
            s = jnp.maximum(jnp.max(jnp.abs(wb), axis=-1, keepdims=True) / qmax, 1e-12)
            wq = jnp.clip(jnp.round(wb / s), -qmax - 1.0, qmax) * s
            return wq.reshape(O, I)
        x = act_qdq(x)
        up = act_qdq(x @ lpbq_dequant(w_up).T)
        gate = act_qdq(x @ lpbq_dequant(w_gate).T)
        sig = fixed_qdq_u16(jax.nn.sigmoid(gate))
        gate = act_qdq(gate * sig)
        o = act_qdq(gate * up)
        return o @ lpbq_dequant(w_down).T
    x = x + jnp.tanh(g_xattn[0]) * _L0_xattn_ref(_layernorm(x, axis=-1), ctx_1024, ctx_1024, L0_xattn_Wq, L0_xattn_Wk, L0_xattn_Wv, L0_xattn_Wo)
    x = x + jnp.tanh(g_ffn[0]) * _L0_ffn_ref(_layernorm(x, axis=-1), L0_ffn_w_gate, L0_ffn_w_up, L0_ffn_w_down)
    return x

_drawn_inputs = setup_inputs


def setup_inputs(seed=0):
    import zlib

    import numpy as np

    out = dict(_drawn_inputs(seed))
    spreads = {}
    factors = {}
    for name, (base, spread) in spreads.items():
        noise = np.random.default_rng([zlib.crc32(name.encode()), seed]).standard_normal(out[name].shape)
        drawn = base * np.exp(spread * noise) if base else spread * noise
        out[name] = jnp.asarray(drawn.astype(out[name].dtype))
    for name, factor in factors.items():
        out[name] = (out[name] * factor).astype(out[name].dtype)
    return out
```

```python
import concourse.bass as bass
from concourse import mybir
from contextlib import ExitStack

F32 = mybir.dt.float32
F32R = mybir.dt.float32r
ALU = mybir.AluOpType
ACT = mybir.ActivationFunctionType
AX = mybir.AxisListType

S = 2048
T = 1601
M = 256
H = 16
D = 64
F = 768
BLOCK = 32
P = 128

KT = M // P
FT = F // P
PAIRS = H // 2
CHUNK = 512
CHUNKS = S // CHUNK
TOK = S // P
TT = -(-T // P)
TLAST = T - (TT - 1) * P
TE = T + 1
STEPS = CHUNKS * TT
HALF = 400
MPIECES = [(0, HALF), (HALF, HALF), (2 * HALF, HALF + 2), (TE - HALF - 2, HALF + 2)]
UNITS = TOK * 2
RING = 4
SCALE = float(D) ** -0.5
EPS = 1e-5
ROUND = 1.5 * 2.0 ** 23
QMAX = 2.0 ** 15 - 1
WMAX = 2.0 ** 3 - 1
TINY = 1e-12
SIG = 65536.0

N_TURNED = 35
X, GATE, UP, GS, OUT = range(5)

OUT3 = ["D3'", "Oa3'", "Ob3'"]
PREP = [f"Q{c}" for c in range(4)] + [f"K{c}" for c in range(4)] + [f"V{c}" for c in range(4)]
FULL = {1: "D3'", 2: "Oa3'", 3: "Ob3'", 4: "Q0", 5: "Q1", 6: "Q2", 7: "Q3", 8: "K0", 9: "K1", 10: "K2",
        11: "K3", 12: "V0", 14: "D0", 16: "Oa0", 17: "Ob0", 18: "V1", 19: "V2", 20: "V3",
        27: "D1", 29: "Oa1", 30: "Ob1", 35: "T0", 40: "D2", 42: "Oa2", 43: "Ob2", 50: "T1"}
ORDER = [FULL[i] for i in sorted(FULL)]
PROLOGUE = PREP + ["T0", "T1"]
M_FIRST, M_LAST = 13, 49


def at_step(i, first, last):
    name = FULL.get(i)
    if name is None or (first and name in OUT3) or (last and name[0] in "QKVT"):
        return None
    return name


def desk_before(p, name):
    if isinstance(p, int) and p == -1:
        return PROLOGUE.index(name)
    done = len(PROLOGUE) - len(OUT3)
    order = ORDER
    if isinstance(p, int) and p >= PAIRS - 1:
        order = [n for n in ORDER if n[0] not in "QKVT"]
        if p == PAIRS:
            return done + len(ORDER) * (PAIRS - 1) + len(order) + OUT3.index(name)
    return p * len(ORDER) + (done + order.index(name))


def units_at(i):
    n = 2 * UNITS
    w = M_LAST - M_FIRST + 1
    if not M_FIRST <= i <= M_LAST:
        return []
    return list(range((i - M_FIRST) * n // w, (i + 1 - M_FIRST) * n // w))


def gated_block(nc, x, ctx, g_xattn, g_ffn, wq, wk, wv, wo, w_gate, w_up, w_down, out):
    whole = ExitStack()
    with whole:
        def sem(name):
            return whole.enter_context(nc.semaphore(name))

        def keep(name, shape, dt=F32):
            return whole.enter_context(nc.sbuf_tensor(name, shape, dt))

        xacc = keep("xacc", [P, TOK, M])
        ident = keep("ident", [P, P])
        ones = keep("ones", [P, D])
        gates = keep("gates", [P, 2])
        tg = keep("tg", [P, 2])
        st = keep("st", [P, TOK, 6])
        mv = keep("mv", [P, TOK, 2])
        sd = keep("sd", [P, TOK])
        rs = keep("rs", [P, TOK])
        epst = keep("epst", [P, 1])
        ones1 = keep("ones1", [1, P])
        lanes = keep("lanes", [P, 5, 6])
        part = keep("part", [P, 5])
        big = keep("big", [1, 5])
        unit = keep("unit", [1, 5])
        raw = keep("raw", [1, 5])
        inv = keep("inv", [1, 5])
        sc1 = keep("sc1", [1, 5, 2])
        scb = keep("scb", [P, 5, 2])
        ring = keep("ring", [P, RING, 2 * CHUNK])
        xn = ring[:, :, :].rearrange("p r (a m) -> p (r a) m", m=M)

        att = ExitStack()

        def sb(name, shape, dt=F32):
            return att.enter_context(nc.sbuf_tensor(name, shape, dt))

        q_hl = [[sb(f"q_hl{b}{h}", [P, S], F32R) for h in range(2)] for b in range(2)]
        q_hm = [[sb(f"q_hm{b}{h}", [P, S], F32R) for h in range(2)] for b in range(2)]
        k_hh = [[sb(f"k_hh{b}{h}", [P, TE], F32R) for h in range(2)] for b in range(2)]
        k_l1 = [[sb(f"k_l1{b}{h}", [P, TE], F32R) for h in range(2)] for b in range(2)]
        v_pair = [sb(f"v_pair{b}", [P, TT, P]) for b in range(2)]
        ctx_nat = [v_pair[b][:, :, :] for b in range(2)]
        xnT = sb("xnT", [P, KT, S])
        ctxT = sb("ctxT", [P, KT, TE])
        psum_p = sb("psum_p", [P, 2 * CHUNK])
        o_sb = sb("o_sb", [P, 2, CHUNK])
        rden = sb("rden", [P, CHUNK])
        w_qkv = [sb(f"w_{n}", [P, KT, P]) for n in "qkv"]
        w_o = sb("w_o", [P, M])
        mx = sb("mx", [P, 2, TOK, 2])
        nm = sb("nm", [P, 2, TOK])
        nmT = [sb(f"nmT{h}", [TOK, P], F32R) for h in range(2)]
        att.close()

        ffn = ExitStack()

        def sf(name, shape, dt=F32):
            return ffn.enter_context(nc.sbuf_tensor(name, shape, dt))

        gate = sf("gate", [P, FT, S])
        up = sf("up", [P, FT, S])
        xqT = sf("xqT", [P, KT, S])
        w_nat = sf("w_nat", [P, 3 * FT, M])
        wg_up = sf("wg_up", [P, 2, KT, F])
        w_dn = sf("w_dn", [P, FT, M])
        sig = [sf(f"sig{b}", [P, S]) for b in range(2)]
        wmax = sf("wmax", [P, 3 * FT * M // BLOCK])
        wsc = sf("wsc", [P, 3 * FT * M // BLOCK])
        winv = sf("winv", [P, 3 * FT * M // BLOCK])
        ffn.close()

        sc = [whole.enter_context(nc.psum_tensor(f"scores{b}", [P, 2 * CHUNK], F32)) for b in range(2)]
        mb = whole.enter_context(nc.psum_tensor("mb", [P, 2 * CHUNK], F32))
        ob = whole.enter_context(nc.psum_tensor("ob", [P, CHUNK], F32))
        desk = whole.enter_context(nc.psum_tensor("desk", [P, CHUNK], F32))
        quad = [sc[n // 2][:, (n % 2) * CHUNK:(n % 2 + 1) * CHUNK] for n in range(4)]
        mring = [mb, sc[0], sc[1]]

        x_in = [sem(f"x_in{c}") for c in range(4)]
        ctx_in, g_in = sem("ctx_in"), sem("g_in")
        w_in, wo_in, shift_in = sem("w_in"), sem("wo_in"), sem("shift_in")
        consts, ident0 = sem("consts"), sem("ident0")
        stats, sd_ready, rs_ready, xn_ready = sem("stats"), sem("sd_ready"), sem("rs_ready"), sem("xn_ready")
        tg_ready = sem("tg_ready")
        turned = sem("turned")
        took_act, took_dve = sem("took_act"), sem("took_dve")
        desk_full, desk_free = sem("desk_full"), sem("desk_free")
        hi_ready, dup_ready = sem("hi_ready"), sem("dup_ready")
        max_full, max_free, nm_ready = sem("max_full"), sem("max_free"), sem("nm_ready")
        sc_full, exp_done, pv_done = sem("sc_full"), sem("exp_done"), sem("pv_done")
        add_a, add_b = sem("add_a"), sem("add_b")
        o_copied, o_ready = sem("o_copied"), sem("o_ready")
        wf_in, w_step = sem("wf_in"), sem("w_step")
        ln_stats = sem("ln_stats")
        lane_max = sem("lane_max")
        gm_part, gm_row, gm_step, gm_bc, gm_ready = (
            sem(f"gm_{n}") for n in ("part", "row", "step", "bc", "ready"))
        x_rnd, xq_ready = sem("x_rnd"), sem("xq_ready")
        fg_full, fg_free = sem("fg_full"), sem("fg_free")
        g_rnd, g_int, sg_ready = sem("g_rnd"), sem("g_int"), sem("sg_ready")
        s_rnd, s_int, gs_ready = sem("s_rnd"), sem("s_int"), sem("gs_ready")
        gs_rnd, gs_int, u_rnd = sem("gs_rnd"), sem("gs_int"), sem("u_rnd")
        o_prod, o_rnd, o_quant = sem("o_prod"), sem("o_rnd"), sem("o_quant")
        dn_full, dn_free, y_out = sem("dn_full"), sem("dn_free"), sem("y_out")

        wq_v, wk_v, wv_v = (w.rearrange("(a h) (c p) d -> a p c h d", h=2, p=P) for w in (wq, wk, wv))
        wo_v = wo.rearrange("(a p) n -> a p n", p=P)
        x_v = x[0].rearrange("(j p) m -> p j m", p=P)
        out_v = out[0].rearrange("(j p) m -> p j m", p=P)

        def turned_from(n):
            if n < 8:
                kt, c = n // 4, n % 4
                tiles = range(4 * c, min(4 * c + 4, TT))
                return [(ctx_nat[kt][0:key_tile(t), t, :], key_tile(t)) for t in tiles], ctx_in, 64
            if n < 24:
                kt, c = n % 8 // 4, n % 4
                src = [(xn[:, 4 * c + j, kt * P:(kt + 1) * P], P) for j in range(4)]
                return (src, xn_ready, 4 * c + 4) if n < 16 else (src, xq_ready, c + 1)
            n -= 24
            if n < 8:
                base, kt, g = n // 4 * FT, n % 4 // 2, n % 2
                return [(w_nat[:, base + 3 * g + j, kt * P:(kt + 1) * P], P) for j in range(3)], w_step, 6
            w_o_nat = w_nat[:, 2 * FT:3 * FT, :].rearrange("p (o a) m -> p o (a m)", o=M // P)
            return [(w_o_nat[:, o, k * P:(k + 1) * P], P)
                    for k in (2 * (n - 8), 2 * (n - 8) + 1) for o in range(M // P)], w_step, 6

        def turned_to(n):
            kt, c = n % 8 // 4, n % 4
            if n < 24:
                dst = ctxT if n < 8 else xnT if n < 16 else xqT
                if n < 8 and c == 3:
                    return ctxT[:, kt, c * CHUNK:T], TLAST, ctxT[:, kt, T:TE]
                return dst[:, kt, c * CHUNK:(c + 1) * CHUNK], CHUNK
            n -= 24
            if n < 8:
                return wg_up[:, n // 4, n % 4 // 2, 3 * P * (n % 2):3 * P * (n % 2 + 1)], 3 * P
            return w_dn[:, 2 * (n - 8):2 * (n - 8) + 2, :].rearrange("p a m -> p (a m)"), CHUNK

        def key_tile(t):
            return TLAST if t == TT - 1 else P

        def k_cols(c):
            return c * CHUNK, min(CHUNK, TE - c * CHUNK)

        block = whole.enter_context(nc.Block())

        @block.sync
        def _(sp):
            for c in range(4):
                sp.dma_start(xacc[:, 4 * c:4 * c + 4, :], x_v[:, 4 * c:4 * c + 4, :]).then_inc(x_in[c], 16)
            for b in range(KT):
                sp.dma_start(ctx_nat[b][:, 0:TT - 1, :],
                             ctx[0, 0:(TT - 1) * P, b * P:(b + 1) * P].rearrange("(j p) m -> p j m", p=P))\
                  .then_inc(ctx_in, 16)
                sp.dma_start(ctx_nat[b][0:TLAST, TT - 1, :], ctx[0, (TT - 1) * P:T, b * P:(b + 1) * P])\
                  .then_inc(ctx_in, 16)
            sp.dma_start(gates[:, 0:1], g_xattn.unsqueeze(0).broadcast_to([P, 1])).then_inc(g_in, 16)
            sp.dma_start(gates[:, 1:2], g_ffn.unsqueeze(0).broadcast_to([P, 1])).then_inc(g_in, 16)

            def load_qkv(q):
                for dst, src in zip(w_qkv, (wq_v, wk_v, wv_v)):
                    for h in range(2):
                        sp.dma_start(dst[:, :, h * D:(h + 1) * D], src[q, :, :, h, :]).then_inc(w_in, 16)

            def send_shift(p, h, b):
                sp.wait_ge(desk_free, desk_before(p, f"T{h}") + 1)
                sp.dma_start(q_hm[b][h][D:D + 1, :].bitcast(F32), nmT[h][:, :].bitcast(F32)).then_inc(shift_in, 16)

            def window(p, b, first=False, last=False):
                if not last:
                    load_qkv(p + 1)
                if not first:
                    sp.wait_ge(desk_full, desk_before(p, "Ob3'") + 1)
                    sp.dma_start(w_o[:, :], wo_v[p]).then_inc(wo_in, 16)
                if not last:
                    for h in range(2):
                        send_shift(p, h, 1 - b)

            load_qkv(0)
            sp.dma_start(w_o[:, :], wo_v[0]).then_inc(wo_in, 16)
            for h in range(2):
                send_shift(-1, h, 0)
            window(0, 0, first=True)
            with sp.Fori(0, PAIRS // 2 - 1) as n:
                window(1 + 2 * n, 1)
                window(2 + 2 * n, 0)
            window(PAIRS - 1, 1, last=True)
            sp.wait_ge(desk_free, desk_before(PAIRS, "Ob3'") + 1)
            sp.dma_start(w_nat[:, 0:FT, :], w_gate.rearrange("(j p) m -> p j m", p=P)).then_inc(wf_in, 16)
            sp.dma_start(w_nat[:, FT:2 * FT, :], w_up.rearrange("(j p) m -> p j m", p=P)).then_inc(wf_in, 16)
            sp.dma_start(w_nat[:, 2 * FT:3 * FT, :].rearrange("p (o a) m -> p o (a m)", o=M // P),
                         w_down.rearrange("(o p) m -> p o m", p=P)).then_inc(wf_in, 16)
            for c in range(4):
                sp.wait_ge(dn_free, 4 * c + 4)
                sp.dma_start(out_v[:, 4 * c:4 * c + 4, :], xacc[:, 4 * c:4 * c + 4, :]).then_inc(y_out, 16)
            sp.wait_ge(y_out, 64)

        @block.gpsimd
        def _(pool):
            nc.gpsimd.memset(ident[:, :], 0.0).then_inc(ident0, 1)
            nc.gpsimd.memset(ones[:, :], 1.0)
            nc.gpsimd.memset(ones1[:, :], 1.0)
            nc.gpsimd.memset(epst[:, :], EPS)
            pool.wait_ge(ident0, 1)
            nc.gpsimd.affine_select(out=ident[:, :], in_=ident[:, :], compare_op=ALU.not_equal, fill=1.0,
                                    base=0, pattern=[[-1, P]], channel_multiplier=1).then_inc(consts, 1)

            def add(p, i):
                t, rows = i % TT, key_tile(i % TT)
                if t == 0:
                    return
                acc = psum_p[0:rows, CHUNK:]
                pool.wait_ge(exp_done, p * STEPS + (i + 1))
                if t == 1:
                    name, q = ("D3'", p) if i < TT else (f"D{i // TT - 1}", p)
                    if not (isinstance(p, int) and p == 0 and i < TT):
                        pool.wait_ge(desk_full, desk_before(q, name) + 1)
                    nc.gpsimd.tensor_tensor(acc, ring[:, (i - 1) % RING, CHUNK:], ring[:, i % RING, CHUNK:],
                                            ALU.add).then_inc(add_b, 2)
                else:
                    pool.wait_ge(add_b, p * STEPS + i)
                    nc.gpsimd.tensor_tensor(acc, acc, ring[0:rows, i % RING, CHUNK:], ALU.add)\
                      .then_inc(add_b, 1)

            def window(p):
                for i in range(STEPS):
                    add(p, i)

            window(0)
            with pool.Fori(0, PAIRS // 2 - 1) as n:
                window(1 + 2 * n)
                window(2 + 2 * n)
            window(PAIRS - 1)

        @block.scalar
        def _(act):
            act.wait_ge(stats, TOK)
            act.wait_ge(consts, 1)
            nc.scalar.activation(sd[:, :], mv[:, :, 1], ACT.Sqrt, bias=epst[:, :]).then_inc(sd_ready, 1)
            act.wait_ge(g_in, 32)
            nc.scalar.activation(tg[:, :], gates[:, :], ACT.Tanh).then_inc(tg_ready, 1)

            def take_turned(n, dst, cols, extra=None):
                act.wait_ge(turned, n + 1)
                last = nc.scalar.activation(dst, quad[n % 4][:, 0:cols], ACT.Copy)
                if extra is not None:
                    last = nc.scalar.activation(extra, quad[n % 4][:, cols - 1:cols], ACT.Copy)
                last.then_inc(took_act, 1)

            for n in range(0, 16, 2):
                take_turned(n, *turned_to(n))

            def desk_piece(p, name, b):
                k = name[0]
                n = int(name[1]) if k in "QKVT" else 0
                if k in "QK":
                    act.wait_ge(desk_full, desk_before(p, name) + 1)
                    c0, w = (n * CHUNK, CHUNK) if k == "Q" else k_cols(n)
                    dst = q_hl if k == "Q" else k_hh
                    nc.scalar.activation(dst[b][0][0:D, c0:c0 + w], desk[0:D, 0:w], ACT.Copy)
                    nc.scalar.activation(dst[b][1][0:D, c0:c0 + w], desk[D:P, 0:w], ACT.Copy)\
                      .then_inc(hi_ready, 1)
                if k == "K" and n == 3:
                    act.wait_ge(hi_ready, (p + 1) * 8 + 8)
                    for h in range(2):
                        nc.scalar.activation(k_hh[b][h][D:P, :], k_hh[b][h][0:D, :].bitcast(F32), ACT.Copy)
                        nc.scalar.activation(q_hm[b][h][0:D, :], q_hl[b][h][0:D, :].bitcast(F32), ACT.Copy)\
                          .then_inc(dup_ready, 1)
                if k == "V":
                    act.wait_ge(desk_full, desk_before(p, name) + 1)
                    if n < 3:
                        nc.scalar.activation(v_pair[b][:, 4 * n:4 * n + 4, :],
                                             desk[:, :].rearrange("p (a d) -> p a d", d=P), ACT.Copy)\
                          .then_inc(desk_free, 1)
                    else:
                        nc.scalar.activation(v_pair[b][0:TLAST, TT - 1, :], desk[0:TLAST, 0:P], ACT.Copy)\
                          .then_inc(desk_free, 1)
                if k == "T":
                    act.wait_ge(desk_full, desk_before(p, name) + 1)
                    if not (isinstance(p, int) and p == -1):
                        act.wait_ge(shift_in, p * 32 + 32)
                    nc.scalar.activation(nmT[n][:, :], desk[0:TOK, 0:P], ACT.Copy).then_inc(desk_free, 1)

            for name in PROLOGUE:
                desk_piece(-1, name, 0)

            def exp(p, i):
                rows = key_tile(i % TT)
                act.wait_ge(sc_full, p * STEPS + (i + 1))
                if not (isinstance(p, int) and p == 0 and i < RING):
                    act.wait_ge(pv_done, p * STEPS + (i - RING + 1))
                    act.wait_ge(add_a, p * STEPS + (i - RING + 1))
                    act.wait_ge(add_b, p * STEPS + (i - RING + 1))
                nc.scalar.activation(ring[0:rows, i % RING, :], sc[i % 2][0:rows, :], ACT.Exp, scale=SCALE)\
                  .then_inc(exp_done, 1)

            def copy_o(p, c):
                act.wait_ge(pv_done, p * STEPS + TT * (c + 1))
                if c < 2:
                    if not (isinstance(p, int) and p == 0):
                        act.wait_ge(desk_full, desk_before(p - 1, "Ob2") + 1 if c == 0 else desk_before(p, "Ob3'") + 1)
                else:
                    act.wait_ge(desk_full, desk_before(p, f"Ob{c - 2}") + 1)
                nc.scalar.activation(o_sb[:, c % 2, :], ob[:, :], ACT.Copy).then_inc(o_copied, 1)

            def window(p, b, first=False, last=False):
                for i in range(STEPS):
                    exp(p, i)
                    name = at_step(i, first, last)
                    if name:
                        desk_piece(p, name, 1 - b)
                    if i and i % TT == 0:
                        copy_o(p, i // TT - 1)
                copy_o(p, CHUNKS - 1)

            window(0, 0, first=True)
            with act.Fori(0, PAIRS // 2 - 1) as n:
                window(1 + 2 * n, 1)
                window(2 + 2 * n, 0)
            window(PAIRS - 1, 1, last=True)

            act.wait_ge(stats, 2 * TOK)
            nc.scalar.activation(sd[:, :], mv[:, :, 1], ACT.Sqrt, bias=epst[:, :]).then_inc(sd_ready, 1)
            for n in range(16, N_TURNED, 2):
                take_turned(n, *turned_to(n))

            def take_product(n):
                dst, m = (gate, n) if n < 4 * FT else (up, n - 4 * FT)
                act.wait_ge(fg_full, n + 1)
                nc.scalar.activation(dst[:, m // 4, m % 4 * CHUNK:(m % 4 + 1) * CHUNK], quad[n % 4], ACT.Copy)\
                   .then_inc(fg_free, 1)

            for n in range(4 * FT):
                take_product(n)
            for it in range(FT):
                for c in range(4):
                    take_product(4 * FT + 4 * it + c)
                act.wait_ge(g_rnd, it + 1)
                nc.scalar.activation(gate[:, it, :], gate[:, it, :], ACT.Copy, bias=-ROUND).then_inc(g_int, 1)
                act.wait_ge(g_int, it + 1)
                if it >= 2:
                    act.wait_ge(gs_ready, it - 1)
                nc.scalar.activation(sig[it % 2][:, :], gate[:, it, :], ACT.Sigmoid,
                                     scale=scb[:, GATE, 0:1]).then_inc(sg_ready, 1)
            act.wait_ge(gm_ready, UP + 1)
            for it in range(FT):
                nc.scalar.activation(up[:, it, :], up[:, it, :], ACT.Copy, bias=ROUND,
                                     scale=scb[:, UP, 1:2]).then_inc(u_rnd, 1)
            act.wait_ge(gm_ready, OUT + 1)
            for it in range(FT):
                nc.scalar.activation(gate[:, it, :], gate[:, it, :], ACT.Copy, bias=ROUND,
                                     scale=scb[:, OUT, 1:2]).then_inc(o_rnd, 1)

        @block.vector
        def _(dve):
            for b in range(2):
                for h in range(2):
                    nc.vector.memset(k_l1[b][h][D:D + 1, :].bitcast(F32), 1.0)

            def layernorm_stats(base):
                for j in range(TOK):
                    if base == 0 and j % 4 == 0:
                        dve.wait_ge(x_in[j // 4], 16)
                    nc.vector.bn_stats(st[:, j, :], xacc[:, j, :]).then_inc(ln_stats, 1)
                for j in range(TOK):
                    dve.wait_ge(ln_stats, base + j + 1)
                    nc.vector.bn_aggr(mv[:, j, :], st[:, j, :]).then_inc(stats, 1)

            def layernorm(base, n):
                dve.wait_ge(sd_ready, n)
                nc.vector.reciprocal(rs[:, :], sd[:, :]).then_inc(rs_ready, 1)
                dve.wait_ge(rs_ready, n)
                for j in range(TOK):
                    nc.vector.tensor_scalar(xn[:, j, :], xacc[:, j, :], mv[:, j, 0:1], rs[:, j:j + 1],
                                            ALU.subtract, ALU.mult).then_inc(xn_ready, 1)

            layernorm_stats(0)
            layernorm(0, 1)

            def take_turned(n, dst, cols, extra=None):
                dve.wait_ge(turned, n + 1)
                last = nc.vector.tensor_copy(dst, quad[n % 4][:, 0:cols])
                if extra is not None:
                    last = nc.vector.tensor_copy(extra, quad[n % 4][:, cols - 1:cols])
                last.then_inc(took_dve, 1)

            for n in range(1, 16, 2):
                take_turned(n, *turned_to(n))

            def split_low(p, name, b):
                n = int(name[1])
                c0, w = (n * CHUNK, CHUNK) if name[0] == "Q" else k_cols(n)
                dve.wait_ge(hi_ready, (p + 1) * 8 + ("QK".index(name[0]) * 4 + n + 1))
                for h in range(2):
                    if name[0] == "Q":
                        hi, lo = q_hl[b][h][0:D, c0:c0 + w], q_hl[b][h][D:P, c0:c0 + w]
                    else:
                        hi, lo = k_hh[b][h][0:D, c0:c0 + w], k_l1[b][h][0:D, c0:c0 + w]
                    last = nc.vector.tensor_tensor(lo, desk[h * D:(h + 1) * D, 0:w], hi.bitcast(F32),
                                                   ALU.subtract)
                last.then_inc(desk_free, 1)

            def unit_max(q, n, deep):
                bank = mring[n % 3] if deep else mb
                h, j, u = n // UNITS, n % UNITS // 2, n % 2
                w = MPIECES[2 * u][1]
                dve.wait_ge(max_full, q * 2 * UNITS + (n + 1))
                nc.vector.tensor_reduce(mx[:, h, j, u:u + 1],
                                        bank[:, :].rearrange("p (a k) -> p a k", a=2)[:, :, 0:w],
                                        AX.XY, ALU.max).then_inc(max_free, 1)
                if n % UNITS == UNITS - 1:
                    dve.wait_ge(max_free, q * 2 * UNITS + (n + 1))
                    nc.vector.tensor_reduce(nm[:, h, :], mx[:, h, :, :], AX.X, ALU.max, negate=True)\
                      .then_inc(nm_ready, 1)

            def add(p, i):
                t, rows = i % TT, key_tile(i % TT)
                if t == 0:
                    return
                acc = psum_p[0:rows, 0:CHUNK]
                dve.wait_ge(exp_done, p * STEPS + (i + 1))
                if t == 1:
                    if not (isinstance(p, int) and p == 0 and i < TT):
                        dve.wait_ge(desk_full, desk_before(p, "D3'" if i < TT else f"D{i // TT - 1}") + 1)
                    nc.vector.tensor_tensor(acc, ring[:, (i - 1) % RING, 0:CHUNK], ring[:, i % RING, 0:CHUNK],
                                            ALU.add).then_inc(add_a, 2)
                else:
                    dve.wait_ge(add_a, p * STEPS + i)
                    nc.vector.tensor_tensor(acc, acc, ring[0:rows, i % RING, 0:CHUNK], ALU.add)\
                      .then_inc(add_a, 1)

            def desk_piece(p, name, b):
                k = name[0]
                prev = name.endswith("'")
                if k in "QK":
                    split_low(p, name, b)
                if k == "D":
                    c = int(name[1])
                    done = (p - 1 if prev else p) * CHUNKS + c
                    if not (isinstance(p, int) and p == 0 and c == 0):
                        dve.wait_ge(o_ready, done)
                    dve.wait_ge(desk_full, desk_before(p, name) + 1)
                    nc.vector.reciprocal(rden[:, :], desk[:, :]).then_inc(desk_free, 1)
                    dve.wait_ge(desk_free, desk_before(p, name) + 1)
                    dve.wait_ge(o_copied, done + 1)
                    nc.vector.tensor_tensor(o_sb[:, c % 2, :], o_sb[:, c % 2, :], rden[:, :], ALU.mult)\
                      .then_inc(o_ready, 1)
                if k == "O":
                    c, u = int(name[2]), "ab".index(name[1])
                    dve.wait_ge(desk_full, desk_before(p, name) + 1)
                    dst = xacc[:, 4 * c + 2 * u:4 * c + 2 * u + 2, :]
                    nc.vector.scalar_tensor_tensor(out=dst, in0=desk[:, :].rearrange("p (a m) -> p a m", m=M),
                                                   scalar=tg[:, 0:1], in1=dst, op0=ALU.mult, op1=ALU.add)\
                      .then_inc(desk_free, 1)

            for name in PREP:
                desk_piece(-1, name, 0)
            for n in range(2 * UNITS):
                unit_max(0, n, True)

            def window(p, b, first=False, last=False):
                for i in range(STEPS):
                    units = [] if last else units_at(i)
                    for n in units[:1]:
                        unit_max(p + 1, n, False)
                    if i:
                        add(p, i - 1)
                    for n in units[1:]:
                        unit_max(p + 1, n, False)
                    name = at_step(i, first, last)
                    if name:
                        desk_piece(p, name, 1 - b)
                add(p, STEPS - 1)

            dve.wait_ge(tg_ready, 1)
            window(0, 0, first=True)
            with dve.Fori(0, PAIRS // 2 - 1) as n:
                window(1 + 2 * n, 1)
                window(2 + 2 * n, 0)
            window(PAIRS - 1, 1, last=True)
            for name in OUT3:
                desk_piece(PAIRS, name, 0)

            dve.wait_ge(desk_free, desk_before(PAIRS, "Ob3'") + 1)
            layernorm_stats(TOK)
            layernorm(TOK, 2)

            def lane_maxima(n, it, src, axis=AX.X):
                nc.vector.tensor_reduce(lanes[:, n, it:it + 1], src, axis, ALU.max,
                                        apply_absolute_value=True).then_inc(lane_max, 1)

            def global_scale(n, tiles):
                dve.wait_ge(lane_max, {X: 4, GATE: 10, UP: 22, GS: 22, OUT: 28}[n])
                nc.vector.tensor_reduce(part[:, n:n + 1], lanes[:, n, 0:tiles], AX.X, ALU.max).then_inc(gm_part, 1)
                if n == GS:
                    nc.vector.tensor_scalar(unit[:, n:n + 1], sc1[:, GATE, 0:1], 1.0 / SIG, None, ALU.mult)\
                      .then_inc(gm_step, 1)
                elif n == OUT:
                    nc.vector.tensor_tensor(unit[:, n:n + 1], sc1[:, UP, 0:1], sc1[:, GS, 0:1], ALU.mult)\
                      .then_inc(gm_step, 1)
                else:
                    nc.vector.memset(unit[:, n:n + 1], 1.0).then_inc(gm_step, 1)
                dve.wait_ge(gm_row, n + 1)
                nc.vector.tensor_reduce(big[:, n:n + 1], mb[0:1, 0:P], AX.X, ALU.max).then_inc(gm_step, 1)
                dve.wait_ge(gm_step, 6 * n + 2)
                nc.vector.tensor_scalar(raw[:, n:n + 1], big[:, n:n + 1], unit[:, n:n + 1], 1.0 / QMAX,
                                        ALU.mult, ALU.mult).then_inc(gm_step, 1)
                dve.wait_ge(gm_step, 6 * n + 3)
                nc.vector.tensor_scalar(sc1[:, n, 0:1], raw[:, n:n + 1], TINY, None, ALU.max).then_inc(gm_step, 1)
                dve.wait_ge(gm_step, 6 * n + 4)
                nc.vector.reciprocal(inv[:, n:n + 1], sc1[:, n, 0:1]).then_inc(gm_step, 1)
                dve.wait_ge(gm_step, 6 * n + 5)
                nc.vector.tensor_tensor(sc1[:, n, 1:2], inv[:, n:n + 1], unit[:, n:n + 1], ALU.mult)\
                  .then_inc(gm_step, 1)
                dve.wait_ge(gm_bc, n + 1)
                nc.vector.tensor_copy(scb[:, n, :], mb[:, CHUNK:CHUNK + 2]).then_inc(gm_ready, 1)
                dve.wait_ge(gm_ready, n + 1)

            dve.wait_ge(xn_ready, 2 * TOK)
            for c in range(4):
                lane_maxima(X, c, xn[:, 4 * c:4 * c + 4, :], AX.XY)
            global_scale(X, 4)
            for c in range(4):
                xc = xn[:, 4 * c:4 * c + 4, :]
                nc.vector.tensor_scalar(xc, xc, scb[:, X, 1:2], ROUND, ALU.mult, ALU.add).then_inc(x_rnd, 1)
            for c in range(4):
                xc = xn[:, 4 * c:4 * c + 4, :]
                dve.wait_ge(x_rnd, c + 1)
                nc.vector.tensor_scalar(xc, xc, ROUND, scb[:, X, 0:1], ALU.subtract, ALU.mult)\
                  .then_inc(xq_ready, 1)

            wb = w_nat[:, :, :].rearrange("p a (k i) -> p (a k) i", i=BLOCK)
            per_block = [P, 3 * FT * M // BLOCK, BLOCK]
            dve.wait_ge(wf_in, 48)
            nc.vector.tensor_reduce(wmax[:, :], wb, AX.X, ALU.max, apply_absolute_value=True).then_inc(w_step, 1)
            dve.wait_ge(w_step, 1)
            nc.vector.tensor_scalar(wsc[:, :], wmax[:, :], 1.0 / WMAX, TINY, ALU.mult, ALU.max).then_inc(w_step, 1)
            dve.wait_ge(w_step, 2)
            nc.vector.reciprocal(winv[:, :], wsc[:, :]).then_inc(w_step, 1)
            dve.wait_ge(w_step, 3)
            nc.vector.tensor_tensor(wb, wb, winv[:, :].unsqueeze(2).broadcast_to(per_block), ALU.mult)\
              .then_inc(w_step, 1)
            dve.wait_ge(w_step, 4)
            nc.vector.tensor_scalar(wb, wb, ROUND, ROUND, ALU.add, ALU.subtract).then_inc(w_step, 1)
            dve.wait_ge(w_step, 5)
            nc.vector.tensor_tensor(wb, wb, wsc[:, :].unsqueeze(2).broadcast_to(per_block), ALU.mult)\
              .then_inc(w_step, 1)
            for n in range(17, N_TURNED, 2):
                take_turned(n, *turned_to(n))

            for it in range(FT):
                dve.wait_ge(fg_free, 4 * (it + 1))
                lane_maxima(GATE, it, gate[:, it, :])
            global_scale(GATE, FT)
            for it in range(FT):
                nc.vector.tensor_scalar(gate[:, it, :], gate[:, it, :], scb[:, GATE, 1:2], ROUND,
                                        ALU.mult, ALU.add).then_inc(g_rnd, 1)
            for it in range(FT):
                sg = sig[it % 2][:, :]
                dve.wait_ge(sg_ready, it + 1)
                nc.vector.tensor_scalar(sg, sg, SIG, ROUND, ALU.mult, ALU.add).then_inc(s_rnd, 1)
                dve.wait_ge(s_rnd, it + 1)
                nc.vector.tensor_scalar(sg, sg, ROUND, SIG - 1, ALU.subtract, ALU.min).then_inc(s_int, 1)
                dve.wait_ge(fg_free, 4 * FT + 4 * (it + 1))
                lane_maxima(UP, it, up[:, it, :])
                dve.wait_ge(s_int, it + 1)
                nc.vector.tensor_tensor(gate[:, it, :], gate[:, it, :], sg, ALU.mult).then_inc(gs_ready, 1)
                dve.wait_ge(gs_ready, it + 1)
                lane_maxima(GS, it, gate[:, it, :])
            global_scale(UP, FT)
            global_scale(GS, FT)
            for it in range(FT):
                g = gate[:, it, :]
                nc.vector.tensor_scalar(g, g, scb[:, GS, 1:2], ROUND, ALU.mult, ALU.add).then_inc(gs_rnd, 1)
                dve.wait_ge(gs_rnd, it + 1)
                nc.vector.tensor_scalar(g, g, ROUND, None, ALU.subtract).then_inc(gs_int, 1)
                dve.wait_ge(gs_int, it + 1)
                dve.wait_ge(u_rnd, it + 1)
                nc.vector.scalar_tensor_tensor(out=g, in0=up[:, it, :], scalar=ROUND, in1=g,
                                               op0=ALU.subtract, op1=ALU.mult).then_inc(o_prod, 1)
                dve.wait_ge(o_prod, it + 1)
                lane_maxima(OUT, it, g)
            global_scale(OUT, FT)
            for it in range(FT):
                g = gate[:, it, :]
                dve.wait_ge(o_rnd, it + 1)
                nc.vector.tensor_scalar(g, g, ROUND, scb[:, OUT, 0:1], ALU.subtract, ALU.mult)\
                  .then_inc(o_quant, 1)
            for j in range(TOK):
                dve.wait_ge(dn_full, j + 1)
                nc.vector.scalar_tensor_tensor(out=xacc[:, j, :], in0=quad[j % 4][:, 0:M], scalar=tg[:, 1:2],
                                               in1=xacc[:, j, :], op0=ALU.mult, op1=ALU.add).then_inc(dn_free, 1)

        @block.tensor
        def _(pe):
            def mm(out_, lhsT, rhs, start=True, stop=True):
                return nc.tensor.matmul(out_, lhsT, rhs, start=start, stop=stop)

            def turn(n):
                src, ready, value = turned_from(n)
                pe.wait_ge(ready, value)
                if n >= 4:
                    pe.wait_ge(took_act if n % 2 == 0 else took_dve, (n - 4) // 2 + 1)
                at = 0
                for ap, rows in src:
                    last = nc.tensor.transpose(quad[n % 4][:, at:at + rows], ap, ident[0:rows, 0:rows])
                    at += rows
                last.then_inc(turned, 1)

            def desk_piece(p, name, b):
                k = name[0]
                n = int(name[1]) if k in "QKVTD" else 0
                if name == "Q0":
                    pe.wait_ge(w_in, (p + 1) * 96 + 96)
                if k == "D":
                    done = p * STEPS + (0 if name.endswith("'") else TT * (n + 1))
                    pe.wait_ge(add_a, done)
                    pe.wait_ge(add_b, done)
                if k == "O":
                    n = int(name[2])
                    prev = name.endswith("'")
                    pe.wait_ge(o_ready, (p - 1 if prev else p) * CHUNKS + (n + 1))
                    if not prev:
                        pe.wait_ge(wo_in, p * 16 + 16)
                if k == "T":
                    pe.wait_ge(nm_ready, (p + 1) * 2 + (n + 1))
                if not (isinstance(p, int) and p == -1 and name == "Q0"):
                    pe.wait_ge(desk_free, desk_before(p, name))
                if k in "QK":
                    src, w = (xnT, w_qkv[0]) if k == "Q" else (ctxT, w_qkv[1])
                    c0, cols = (n * CHUNK, CHUNK) if k == "Q" else k_cols(n)
                    for kt in range(KT):
                        last = mm(desk[:, 0:cols], w[:, kt, :], src[:, kt, c0:c0 + cols], kt == 0, kt == KT - 1)
                if k == "V":
                    for t in range(4 * n, min(4 * n + 4, TT)):
                        rows = key_tile(t)
                        for kt in range(KT):
                            last = mm(desk[0:rows, (t % 4) * P:(t % 4 + 1) * P], ctxT[:, kt, t * P:t * P + rows],
                                      w_qkv[2][:, kt, :], kt == 0, kt == KT - 1)
                if k == "T":
                    last = nc.tensor.transpose(desk[0:TOK, 0:P], nm[:, n, :], ident[:, :])
                if k == "D":
                    for h in range(2):
                        last = mm(desk[h * D:(h + 1) * D, :], ones[:, :], psum_p[:, h * CHUNK:(h + 1) * CHUNK])
                if k == "O":
                    for j in range(2):
                        tok = (2 * "ab".index(name[1]) + j) * P
                        last = mm(desk[:, j * M:(j + 1) * M], o_sb[:, n % 2, tok:tok + P], w_o[:, :])
                last.then_inc(desk_full, 1)

            def unit_scores(q, n, b, deep):
                bank = mring[n % 3] if deep else mb
                h, j, u = n // UNITS, n % UNITS // 2, n % 2
                if n == 0:
                    pe.wait_ge(dup_ready, q * 2 + 2)
                if deep and n >= 3:
                    pe.wait_ge(max_free, n - 2)
                if not deep:
                    pe.wait_ge(max_free, q * 2 * UNITS + n)
                for a in range(2):
                    k0, w = MPIECES[2 * u + a]
                    last = mm(bank[:, a * CHUNK:a * CHUNK + w], q_hl[b][h][:, j * P:(j + 1) * P],
                              k_hh[b][h][:, k0:k0 + w])
                last.then_inc(max_full, 1)

            def scores(p, i, b):
                c, t = i // TT, i % TT
                rows = key_tile(t)
                if i == 0:
                    pe.wait_ge(shift_in, p * 32 + 32)
                if isinstance(p, int) and p == 0 and i < 2:
                    pe.wait_ge(max_free, 2 * UNITS)
                else:
                    pe.wait_ge(exp_done, p * STEPS + (i - 1))
                for h in range(2):
                    dst = sc[i % 2][0:rows, h * CHUNK:(h + 1) * CHUNK]
                    qs = slice(c * CHUNK, (c + 1) * CHUNK)
                    mm(dst, k_hh[b][h][:, t * P:t * P + rows], q_hl[b][h][:, qs], True, False)
                    last = mm(dst, k_l1[b][h][0:D + 1, t * P:t * P + rows], q_hm[b][h][0:D + 1, qs], False, True)
                last.then_inc(sc_full, 1)

            def values(p, i, b):
                c, t = i // TT, i % TT
                rows = key_tile(t)
                pe.wait_ge(exp_done, p * STEPS + (i + 1))
                if t == 0 and not (isinstance(p, int) and p == 0 and c == 0):
                    pe.wait_ge(o_copied, p * CHUNKS + c)
                for h in range(2):
                    last = mm(ob[h * D:(h + 1) * D, :], v_pair[b][0:rows, t, h * D:(h + 1) * D],
                              ring[0:rows, i % RING, h * CHUNK:(h + 1) * CHUNK], t == 0, t == TT - 1)
                last.then_inc(pv_done, 1)

            def window(p, b, first=False, last=False):
                for i in range(STEPS):
                    scores(p, i, b)
                    units = [] if last else units_at(i)
                    for n in units[:1]:
                        unit_scores(p + 1, n, 1 - b, False)
                    name = at_step(i, first, last)
                    if name:
                        desk_piece(p, name, 1 - b)
                    if i:
                        values(p, i - 1, b)
                    for n in units[1:]:
                        unit_scores(p + 1, n, 1 - b, False)
                values(p, STEPS - 1, b)

            pe.wait_ge(consts, 1)
            for n in range(16):
                turn(n)
            pe.wait_ge(took_act, 8)
            pe.wait_ge(took_dve, 8)
            for name in PREP:
                desk_piece(-1, name, 0)
            for n in range(2 * UNITS):
                unit_scores(0, n, 0, True)
            for name in ("T0", "T1"):
                desk_piece(-1, name, 0)
            window(0, 0, first=True)
            with pe.Fori(0, PAIRS // 2 - 1) as n:
                window(1 + 2 * n, 1)
                window(2 + 2 * n, 0)
            window(PAIRS - 1, 1, last=True)
            for name in OUT3:
                desk_piece(PAIRS, name, 0)

            def find_scale(n):
                pe.wait_ge(gm_part, n + 1)
                mm(mb[0:1, 0:P], part[:, n:n + 1], ident[:, :]).then_inc(gm_row, 1)
                pe.wait_ge(gm_step, 6 * n + 6)
                mm(mb[:, CHUNK:CHUNK + 2], ones1[0:1, :], sc1[0:1, n, :]).then_inc(gm_bc, 1)

            find_scale(X)
            for n in range(16, N_TURNED):
                turn(n)
            pe.wait_ge(took_act, (N_TURNED + 1) // 2)
            pe.wait_ge(took_dve, N_TURNED // 2)

            def product(n):
                m, it, c = n // (4 * FT), n % (4 * FT) // 4, n % 4
                if n >= 4:
                    pe.wait_ge(fg_free, n - 3)
                for kt in range(KT):
                    last = mm(quad[n % 4], wg_up[:, m, kt, it * P:(it + 1) * P],
                              xqT[:, kt, c * CHUNK:(c + 1) * CHUNK], kt == 0, kt == KT - 1)
                last.then_inc(fg_full, 1)

            for n in range(8 * FT):
                product(n)
                if n == 4 * FT + 2:
                    find_scale(GATE)
            for n in (UP, GS, OUT):
                find_scale(n)
            pe.wait_ge(fg_free, 8 * FT)
            for j in range(TOK):
                if j >= 4:
                    pe.wait_ge(dn_free, j - 3)
                for it in range(FT):
                    if j == 0:
                        pe.wait_ge(o_quant, it + 1)
                    last = mm(quad[j % 4][:, 0:M], gate[:, it, j * P:(j + 1) * P], w_dn[:, it, :],
                              it == 0, it == FT - 1)
                last.then_inc(dn_full, 1)


_INS = ["x", "ctx_1024", "g_xattn", "g_ffn", "L0_xattn_Wq", "L0_xattn_Wk", "L0_xattn_Wv", "L0_xattn_Wo",
        "L0_ffn_w_gate", "L0_ffn_w_up", "L0_ffn_w_down"]


def kernel(**inputs):
    import numpy as np
    import concourse.bacc as bacc
    from concourse.bass_utils import run_bass_kernel_spmd as run

    nc = bacc.Bacc("TRN2", target_bir_lowering=False, num_devices=1)
    arrays, args = {}, []
    for name in _INS:
        a = np.ascontiguousarray(inputs[name])
        arrays[f"in_{name}"] = a
        args.append(nc.dram_tensor(f"in_{name}", a.shape, mybir.dt.from_np(a.dtype), kind="ExternalInput").ap())
    args.append(nc.dram_tensor("out_0", (1, S, M), F32, kind="ExternalOutput").ap())
    gated_block(nc, *args)
    r = run(nc, [arrays], core_ids=[0])
    return r.results[0]["out_0"]
```

```python
import concourse.bass as bass
from concourse import mybir
from contextlib import ExitStack

F32 = mybir.dt.float32
F32R = mybir.dt.float32r
ALU = mybir.AluOpType
ACT = mybir.ActivationFunctionType
AX = mybir.AxisListType

S = 2048
T = 1601
M = 256
H = 16
D = 64
F = 768
BLOCK = 32
P = 128

KT = M // P
FT = F // P
PAIRS = H // 2
CHUNK = 512
CHUNKS = S // CHUNK
TOK = S // P
TT = -(-T // P)
TLAST = T - (TT - 1) * P
TE = T + 1
STEPS = CHUNKS * TT
HALF = 400
MPIECES = [(0, HALF), (HALF, HALF), (2 * HALF, HALF + 2), (TE - HALF - 2, HALF + 2)]
UNITS = 2 * (TOK // CHUNKS) * len(MPIECES)
RING = 4
SPLIT = 384
SCALE = float(D) ** -0.5
EPS = 1e-5
ROUND = 1.5 * 2.0 ** 23
QMAX = 2.0 ** 15 - 1
WMAX = 2.0 ** 3 - 1
TINY = 1e-12
SIG = 65536.0

N_TURNED = 35
X, GATE, UP, GS, OUT = range(5)

OUT3 = ["D3'", "Oa3'", "Ob3'"]
PREP = [f"{k}{n}" for k in "QKV" for n in range(4)]
PROLOGUE = PREP + ["T0"]
FULL = {}
for _c in range(CHUNKS):
    _d = "3'" if _c == 0 else str(_c - 1)
    FULL.update({TT * _c + _i: _n for _i, _n in (
        (1, "D" + _d), (2, PREP[3 * _c]), (5, "Oa" + _d), (6, PREP[3 * _c + 1]), (7, "Ob" + _d),
        (9, PREP[3 * _c + 2]), (11, f"T{(_c + 1) % CHUNKS}"))})
UNITS_AT = [2, 3, 4, 1, 1, 2, 5, 3, 3, 5, 3, 0, 0]
QUARTERS = {2 + _q: _q for _q in range(4)}


def desk_order(first=False, last=False):
    return [FULL[i] for i in sorted(FULL)
            if not (first and FULL[i] in OUT3) and not (last and FULL[i] in PREP + ["T0"])]


def at_step(i, first, last):
    return FULL[i] if i in FULL and FULL[i] in desk_order(first, last) else None


def desk_before(p, name):
    if isinstance(p, int) and p == -1:
        return PROLOGUE.index(name)
    if isinstance(p, int) and p == 0:
        return len(PROLOGUE) + desk_order(first=True).index(name)
    each = len(desk_order())
    ahead = len(PROLOGUE) + len(desk_order(first=True)) - each
    if isinstance(p, int) and p == PAIRS:
        return ahead + each * (PAIRS - 1) + len(desk_order(last=True)) + OUT3.index(name)
    return p * each + (ahead + desk_order(last=isinstance(p, int) and p == PAIRS - 1).index(name))


def units_at(i):
    done = sum(UNITS_AT[:i % TT])
    return list(range(done, done + UNITS_AT[i % TT]))


assert sum(UNITS_AT) == UNITS


def gated_block(nc, x, ctx, g_xattn, g_ffn, wq, wk, wv, wo, w_gate, w_up, w_down, out):
    whole = ExitStack()
    with whole:
        def sem(name):
            return whole.enter_context(nc.semaphore(name))

        def keep(name, shape, dt=F32):
            return whole.enter_context(nc.sbuf_tensor(name, shape, dt))

        xacc = keep("xacc", [P, TOK, M])
        ident = keep("ident", [P, P])
        ones = keep("ones", [P, D])
        gates = keep("gates", [P, 2])
        tg = keep("tg", [P, 2])
        st = keep("st", [P, TOK, 6])
        mv = keep("mv", [P, TOK, 2])
        sd = keep("sd", [P, TOK])
        rs = keep("rs", [P, TOK])
        epst = keep("epst", [P, 1])
        ones1 = keep("ones1", [1, P])
        lanes = keep("lanes", [P, 5, 6])
        part = keep("part", [P, 5])
        big = keep("big", [1, 5])
        unit = keep("unit", [1, 5])
        raw = keep("raw", [1, 5])
        inv = keep("inv", [1, 5])
        sc1 = keep("sc1", [1, 5, 2])
        scb = keep("scb", [P, 5, 2])
        ring = keep("ring", [P, RING, 2 * CHUNK])
        xn = ring[:, :, :].rearrange("p r (a m) -> p (r a) m", m=M)

        att = ExitStack()

        def sb(name, shape, dt=F32):
            return att.enter_context(nc.sbuf_tensor(name, shape, dt))

        q_hl = [[sb(f"q_hl{b}{h}", [P, S], F32R) for h in range(2)] for b in range(2)]
        q_hm = [[sb(f"q_hm{b}{h}", [P, S], F32R) for h in range(2)] for b in range(2)]
        k_hh = [[sb(f"k_hh{b}{h}", [P, TE], F32R) for h in range(2)] for b in range(2)]
        k_l1 = [[sb(f"k_l1{b}{h}", [P, TE], F32R) for h in range(2)] for b in range(2)]
        v_pair = [sb(f"v_pair{b}", [P, TT, P]) for b in range(2)]
        ctx_nat = [v_pair[b][:, :, :] for b in range(2)]
        xnT = sb("xnT", [P, KT, S])
        ctxT = sb("ctxT", [P, KT, TE])
        psum_p = sb("psum_p", [P, 2 * CHUNK])
        o_sb = sb("o_sb", [P, 2, CHUNK])
        rden = sb("rden", [P, CHUNK])
        stage = sb("stage", [P, CHUNK])
        w_qkv = [sb(f"w_{n}", [P, KT, P]) for n in "qkv"]
        w_o = sb("w_o", [P, M])
        mx = sb("mx", [P, 2, TOK // CHUNKS, len(MPIECES)])
        nm = sb("nm", [P, 2 * TOK // CHUNKS])
        nmT = sb("nmT", [2 * TOK // CHUNKS, P], F32R)
        att.close()

        ffn = ExitStack()

        def sf(name, shape, dt=F32):
            return ffn.enter_context(nc.sbuf_tensor(name, shape, dt))

        gate = sf("gate", [P, FT, S])
        up = sf("up", [P, FT, S])
        xqT = sf("xqT", [P, KT, S])
        w_nat = sf("w_nat", [P, 3 * FT, M])
        wg_up = sf("wg_up", [P, 2, KT, F])
        w_dn = sf("w_dn", [P, FT, M])
        sig = [sf(f"sig{b}", [P, S]) for b in range(2)]
        wmax = sf("wmax", [P, 3 * FT * M // BLOCK])
        wsc = sf("wsc", [P, 3 * FT * M // BLOCK])
        winv = sf("winv", [P, 3 * FT * M // BLOCK])
        ffn.close()

        sc = [whole.enter_context(nc.psum_tensor(f"scores{b}", [P, 2 * CHUNK], F32)) for b in range(2)]
        mb = whole.enter_context(nc.psum_tensor("mb", [P, 2 * CHUNK], F32))
        ob = whole.enter_context(nc.psum_tensor("ob", [P, CHUNK], F32))
        desk = whole.enter_context(nc.psum_tensor("desk", [P, CHUNK], F32))
        quad = [sc[n // 2][:, (n % 2) * CHUNK:(n % 2 + 1) * CHUNK] for n in range(4)]
        mring = [mb[:, 0:CHUNK], mb[:, CHUNK:]] + quad

        x_in = [sem(f"x_in{c}") for c in range(4)]
        ctx_in, g_in = sem("ctx_in"), sem("g_in")
        w_in, wo_in, shift_in = sem("w_in"), sem("wo_in"), sem("shift_in")
        consts, ident0 = sem("consts"), sem("ident0")
        stats, sd_ready, rs_ready, xn_ready = sem("stats"), sem("sd_ready"), sem("rs_ready"), sem("xn_ready")
        tg_ready = sem("tg_ready")
        turned = sem("turned")
        took_act, took_dve = sem("took_act"), sem("took_dve")
        desk_full, desk_free = sem("desk_full"), sem("desk_free")
        hi_ready, lo_ready, zeroed = sem("hi_ready"), sem("lo_ready"), sem("zeroed")
        max_full, max_free, nm_ready = sem("max_full"), sem("max_free"), sem("nm_ready")
        sc_full, exp_done, pv_done = sem("sc_full"), sem("exp_done"), sem("pv_done")
        add_a, add_b, den_inv = sem("add_a"), sem("add_b"), sem("den_inv")
        o_copied, o_ready = sem("o_copied"), sem("o_ready")
        wf_in, w_step = sem("wf_in"), sem("w_step")
        ln_stats = sem("ln_stats")
        lane_max = sem("lane_max")
        gm_part, gm_row, gm_step, gm_bc, gm_ready = (
            sem(f"gm_{n}") for n in ("part", "row", "step", "bc", "ready"))
        x_rnd, xq_ready = sem("x_rnd"), sem("xq_ready")
        fg_full, fg_free = sem("fg_full"), sem("fg_free")
        g_rnd, g_int, sg_ready = sem("g_rnd"), sem("g_int"), sem("sg_ready")
        s_rnd, s_int, gs_ready = sem("s_rnd"), sem("s_int"), sem("gs_ready")
        gs_rnd, gs_int, u_rnd = sem("gs_rnd"), sem("gs_int"), sem("u_rnd")
        o_prod, o_rnd, o_quant = sem("o_prod"), sem("o_rnd"), sem("o_quant")
        dn_full, dn_free, y_out = sem("dn_full"), sem("dn_free"), sem("y_out")

        wq_v, wk_v, wv_v = (w.rearrange("(a h) (c p) d -> a p c h d", h=2, p=P) for w in (wq, wk, wv))
        wo_v = wo.rearrange("(a p) n -> a p n", p=P)
        x_v = x[0].rearrange("(j p) m -> p j m", p=P)
        out_v = out[0].rearrange("(j p) m -> p j m", p=P)

        def turned_from(n):
            if n < 8:
                kt, c = n // 4, n % 4
                tiles = range(4 * c, min(4 * c + 4, TT))
                return [(ctx_nat[kt][0:key_tile(t), t, :], key_tile(t)) for t in tiles], ctx_in, 64
            if n < 24:
                kt, c = n % 8 // 4, n % 4
                src = [(xn[:, 4 * c + j, kt * P:(kt + 1) * P], P) for j in range(4)]
                return (src, xn_ready, 4 * c + 4) if n < 16 else (src, xq_ready, c + 1)
            n -= 24
            if n < 8:
                base, kt, g = n // 4 * FT, n % 4 // 2, n % 2
                return [(w_nat[:, base + 3 * g + j, kt * P:(kt + 1) * P], P) for j in range(3)], w_step, 6
            w_o_nat = w_nat[:, 2 * FT:3 * FT, :].rearrange("p (o a) m -> p o (a m)", o=M // P)
            return [(w_o_nat[:, o, k * P:(k + 1) * P], P)
                    for k in (2 * (n - 8), 2 * (n - 8) + 1) for o in range(M // P)], w_step, 6

        def turned_to(n):
            kt, c = n % 8 // 4, n % 4
            if n < 24:
                dst = ctxT if n < 8 else xnT if n < 16 else xqT
                if n < 8 and c == 3:
                    return ctxT[:, kt, c * CHUNK:T], TLAST, ctxT[:, kt, T:TE]
                return dst[:, kt, c * CHUNK:(c + 1) * CHUNK], CHUNK
            n -= 24
            if n < 8:
                return wg_up[:, n // 4, n % 4 // 2, 3 * P * (n % 2):3 * P * (n % 2 + 1)], 3 * P
            return w_dn[:, 2 * (n - 8):2 * (n - 8) + 2, :].rearrange("p a m -> p (a m)"), CHUNK

        def key_tile(t):
            return TLAST if t == TT - 1 else P

        def k_cols(c):
            return c * CHUNK, min(CHUNK, TE - c * CHUNK)

        block = whole.enter_context(nc.Block())

        @block.sync
        def _(sp):
            for c in range(4):
                sp.dma_start(xacc[:, 4 * c:4 * c + 4, :], x_v[:, 4 * c:4 * c + 4, :]).then_inc(x_in[c], 16)
            for b in range(KT):
                sp.dma_start(ctx_nat[b][:, 0:TT - 1, :],
                             ctx[0, 0:(TT - 1) * P, b * P:(b + 1) * P].rearrange("(j p) m -> p j m", p=P))\
                  .then_inc(ctx_in, 16)
                sp.dma_start(ctx_nat[b][0:TLAST, TT - 1, :], ctx[0, (TT - 1) * P:T, b * P:(b + 1) * P])\
                  .then_inc(ctx_in, 16)
            sp.dma_start(gates[:, 0:1], g_xattn.unsqueeze(0).broadcast_to([P, 1])).then_inc(g_in, 16)
            sp.dma_start(gates[:, 1:2], g_ffn.unsqueeze(0).broadcast_to([P, 1])).then_inc(g_in, 16)

            def load_qkv(q):
                for dst, src in zip(w_qkv, (wq_v, wk_v, wv_v)):
                    for h in range(2):
                        sp.dma_start(dst[:, :, h * D:(h + 1) * D], src[q, :, :, h, :]).then_inc(w_in, 16)

            def send_shift(p, c, b):
                sp.wait_ge(desk_free, desk_before(p, f"T{c}") + 1)
                for h in range(2):
                    row = slice(D, D + 1) if h == 0 else slice(0, 1)
                    sp.dma_start(q_hm[b][h][row, c * CHUNK:(c + 1) * CHUNK].bitcast(F32),
                                 nmT[4 * h:4 * h + 4, :].bitcast(F32)).then_inc(shift_in, 16)

            def window(p, b, first=False, last=False):
                if not last:
                    load_qkv(p + 1)
                if not first:
                    sp.wait_ge(desk_full, desk_before(p, "Ob3'") + 1)
                    sp.dma_start(w_o[:, :], wo_v[p]).then_inc(wo_in, 16)
                for c in range(1, CHUNKS):
                    send_shift(p, c, b)
                if not last:
                    send_shift(p, 0, 1 - b)

            load_qkv(0)
            sp.dma_start(w_o[:, :], wo_v[0]).then_inc(wo_in, 16)
            send_shift(-1, 0, 0)
            window(0, 0, first=True)
            with sp.Fori(0, PAIRS // 2 - 1) as n:
                window(1 + 2 * n, 1)
                window(2 + 2 * n, 0)
            window(PAIRS - 1, 1, last=True)
            sp.wait_ge(desk_free, desk_before(PAIRS, "Ob3'") + 1)
            sp.dma_start(w_nat[:, 0:FT, :], w_gate.rearrange("(j p) m -> p j m", p=P)).then_inc(wf_in, 16)
            sp.dma_start(w_nat[:, FT:2 * FT, :], w_up.rearrange("(j p) m -> p j m", p=P)).then_inc(wf_in, 16)
            sp.dma_start(w_nat[:, 2 * FT:3 * FT, :].rearrange("p (o a) m -> p o (a m)", o=M // P),
                         w_down.rearrange("(o p) m -> p o m", p=P)).then_inc(wf_in, 16)
            for c in range(4):
                sp.wait_ge(dn_free, 4 * c + 4)
                sp.dma_start(out_v[:, 4 * c:4 * c + 4, :], xacc[:, 4 * c:4 * c + 4, :]).then_inc(y_out, 16)
            sp.wait_ge(y_out, 64)

        @block.gpsimd
        def _(pool):
            nc.gpsimd.memset(ident[:, :], 0.0).then_inc(ident0, 1)
            nc.gpsimd.memset(ones[:, :], 1.0)
            nc.gpsimd.memset(ones1[:, :], 1.0)
            nc.gpsimd.memset(epst[:, :], EPS)
            pool.wait_ge(ident0, 1)
            nc.gpsimd.affine_select(out=ident[:, :], in_=ident[:, :], compare_op=ALU.not_equal, fill=1.0,
                                    base=0, pattern=[[-1, P]], channel_multiplier=1).then_inc(consts, 1)

            def add(p, i):
                t, rows = i % TT, key_tile(i % TT)
                if t == 0:
                    return
                acc = psum_p[0:rows, SPLIT:]
                pool.wait_ge(exp_done, p * STEPS + (i + 1))
                if t == 1:
                    if not (isinstance(p, int) and p == 0 and i < TT):
                        pool.wait_ge(desk_full, desk_before(p, "D3'" if i < TT else f"D{i // TT - 1}") + 1)
                    nc.gpsimd.tensor_tensor(acc, ring[:, (i - 1) % RING, SPLIT:], ring[:, i % RING, SPLIT:],
                                            ALU.add).then_inc(add_b, 2)
                else:
                    pool.wait_ge(add_b, p * STEPS + i)
                    nc.gpsimd.tensor_tensor(acc, acc, ring[0:rows, i % RING, SPLIT:], ALU.add)\
                      .then_inc(add_b, 1)

            def split_low(p, name, b):
                n = int(name[1])
                c0, w = (n * CHUNK, CHUNK) if name[0] == "Q" else k_cols(n)
                cols = slice(c0, c0 + w)
                pool.wait_ge(hi_ready, (p + 1) * 8 + (PREP.index(name) + 1))
                for h in range(2):
                    own = slice(h * D, (h + 1) * D)
                    hi, lo = (q_hm, q_hl) if name[0] == "Q" else (k_hh, k_l1)
                    nc.gpsimd.tensor_tensor(lo[b][h][own, cols], stage[own, 0:w],
                                            hi[b][h][own, cols].bitcast(F32), ALU.subtract).then_inc(lo_ready, 1)
                    pool.wait_ge(lo_ready, (p + 1) * 16 + (2 * PREP.index(name) + h + 1))

            def window(p, b, first=False, last=False):
                for i in range(STEPS):
                    add(p, i)
                    name = at_step(i, first, last)
                    if name and name[0] in "QK":
                        if i % TT:
                            pool.wait_ge(add_b, p * STEPS + (i + 1))
                        split_low(p, name, 1 - b)

            for name in PREP[:8]:
                split_low(-1, name, 0)
            window(0, 0, first=True)
            with pool.Fori(0, PAIRS // 2 - 1) as n:
                window(1 + 2 * n, 1)
                window(2 + 2 * n, 0)
            window(PAIRS - 1, 1, last=True)

        @block.scalar
        def _(act):
            act.wait_ge(stats, TOK)
            act.wait_ge(consts, 1)
            nc.scalar.activation(sd[:, :], mv[:, :, 1], ACT.Sqrt, bias=epst[:, :]).then_inc(sd_ready, 1)
            act.wait_ge(g_in, 32)
            nc.scalar.activation(tg[:, :], gates[:, :], ACT.Tanh).then_inc(tg_ready, 1)

            def take_turned(n, dst, cols, extra=None):
                act.wait_ge(turned, n + 1)
                last = nc.scalar.activation(dst, quad[n % 4][:, 0:cols], ACT.Copy)
                if extra is not None:
                    last = nc.scalar.activation(extra, quad[n % 4][:, cols - 1:cols], ACT.Copy)
                last.then_inc(took_act, 1)

            for n in range(0, 16, 2):
                take_turned(n, *turned_to(n))

            def desk_piece(p, name, b):
                k = name[0]
                n = int(name[1]) if k in "QKVT" else 0
                if k in "QK":
                    c0, w = (n * CHUNK, CHUNK) if k == "Q" else k_cols(n)
                    cols = slice(c0, c0 + w)
                    done = PREP.index(name)
                    act.wait_ge(desk_full, desk_before(p, name) + 1)
                    if not (isinstance(p, int) and p == -1 and done == 0):
                        act.wait_ge(lo_ready, (p + 1) * 16 + 2 * done)
                    nc.scalar.activation(stage[:, 0:w], desk[:, 0:w], ACT.Copy).then_inc(desk_free, 1)
                    act.wait_ge(desk_free, desk_before(p, name) + 1)
                    for h in range(2):
                        for dst, half in ((q_hm, h), (q_hl, 1 - h)) if k == "Q" else ((k_hh, 0), (k_hh, 1)):
                            last = nc.scalar.activation(dst[b][h][half * D:(half + 1) * D, cols],
                                                        stage[h * D:(h + 1) * D, 0:w], ACT.Copy)
                    last.then_inc(hi_ready, 1)
                if k == "V":
                    act.wait_ge(desk_full, desk_before(p, name) + 1)
                    if n < 3:
                        nc.scalar.activation(v_pair[b][:, 4 * n:4 * n + 4, :],
                                             desk[:, :].rearrange("p (a d) -> p a d", d=P), ACT.Copy)\
                          .then_inc(desk_free, 1)
                    else:
                        nc.scalar.activation(v_pair[b][0:TLAST, TT - 1, :], desk[0:TLAST, 0:P], ACT.Copy)\
                          .then_inc(desk_free, 1)
                if k == "T":
                    act.wait_ge(desk_full, desk_before(p, name) + 1)
                    if not (isinstance(p, int) and p == -1):
                        act.wait_ge(shift_in, p * (32 * CHUNKS) + 32 * (n or CHUNKS))
                    nc.scalar.activation(nmT[:, :], desk[0:2 * TOK // CHUNKS, 0:P], ACT.Copy).then_inc(desk_free, 1)
                if k == "D":
                    c = int(name[1])
                    done = (p - 1 if name.endswith("'") else p) * CHUNKS + c
                    if not (isinstance(p, int) and p == 0 and c == 0):
                        act.wait_ge(o_ready, done * 4)
                    act.wait_ge(desk_full, desk_before(p, name) + 1)
                    nc.scalar.activation(rden[:, :], desk[:, :], ACT.Copy).then_inc(desk_free, 1)

            for name in PROLOGUE:
                desk_piece(-1, name, 0)

            def exp(p, i):
                rows = key_tile(i % TT)
                act.wait_ge(sc_full, p * STEPS + (i + 1))
                if not (isinstance(p, int) and p == 0 and i < RING):
                    act.wait_ge(pv_done, p * STEPS + (i - RING + 1))
                    act.wait_ge(add_a, p * STEPS + (i - RING + 1))
                    act.wait_ge(add_b, p * STEPS + (i - RING + 1))
                nc.scalar.activation(ring[0:rows, i % RING, :], sc[i % 2][0:rows, :], ACT.Exp, scale=SCALE)\
                  .then_inc(exp_done, 1)

            def copy_o(p, c):
                act.wait_ge(pv_done, p * STEPS + TT * (c + 1))
                if c < 2:
                    if not (isinstance(p, int) and p == 0):
                        act.wait_ge(desk_full, desk_before(p - 1, "Ob2") + 1 if c == 0 else desk_before(p, "Ob3'") + 1)
                else:
                    act.wait_ge(desk_full, desk_before(p, f"Ob{c - 2}") + 1)
                nc.scalar.activation(o_sb[:, c % 2, :], ob[:, :], ACT.Copy).then_inc(o_copied, 1)

            def window(p, b, first=False, last=False):
                for i in range(STEPS):
                    exp(p, i)
                    name = at_step(i, first, last)
                    if name:
                        desk_piece(p, name, 1 - b)
                    if i and i % TT == 0:
                        copy_o(p, i // TT - 1)
                copy_o(p, CHUNKS - 1)

            window(0, 0, first=True)
            with act.Fori(0, PAIRS // 2 - 1) as n:
                window(1 + 2 * n, 1)
                window(2 + 2 * n, 0)
            window(PAIRS - 1, 1, last=True)
            desk_piece(PAIRS, "D3'", 0)

            act.wait_ge(stats, 2 * TOK)
            nc.scalar.activation(sd[:, :], mv[:, :, 1], ACT.Sqrt, bias=epst[:, :]).then_inc(sd_ready, 1)
            for n in range(16, N_TURNED, 2):
                take_turned(n, *turned_to(n))

            def take_product(n):
                dst, m = (gate, n) if n < 4 * FT else (up, n - 4 * FT)
                act.wait_ge(fg_full, n + 1)
                nc.scalar.activation(dst[:, m // 4, m % 4 * CHUNK:(m % 4 + 1) * CHUNK], quad[n % 4], ACT.Copy)\
                   .then_inc(fg_free, 1)

            for n in range(4 * FT):
                take_product(n)
            for it in range(FT):
                for c in range(4):
                    take_product(4 * FT + 4 * it + c)
                act.wait_ge(g_rnd, it + 1)
                nc.scalar.activation(gate[:, it, :], gate[:, it, :], ACT.Copy, bias=-ROUND).then_inc(g_int, 1)
                act.wait_ge(g_int, it + 1)
                if it >= 2:
                    act.wait_ge(gs_ready, it - 1)
                nc.scalar.activation(sig[it % 2][:, :], gate[:, it, :], ACT.Sigmoid,
                                     scale=scb[:, GATE, 0:1]).then_inc(sg_ready, 1)
            act.wait_ge(gm_ready, UP + 1)
            for it in range(FT):
                nc.scalar.activation(up[:, it, :], up[:, it, :], ACT.Copy, bias=ROUND,
                                     scale=scb[:, UP, 1:2]).then_inc(u_rnd, 1)
            act.wait_ge(gm_ready, OUT + 1)
            for it in range(FT):
                nc.scalar.activation(gate[:, it, :], gate[:, it, :], ACT.Copy, bias=ROUND,
                                     scale=scb[:, OUT, 1:2]).then_inc(o_rnd, 1)

        @block.vector
        def _(dve):
            for b in range(2):
                nc.vector.memset(k_l1[b][0][D:D + 1, :].bitcast(F32), 1.0)
                nc.vector.memset(q_hm[b][1][0:D, :].bitcast(F32), 0.0)
                nc.vector.memset(k_l1[b][1][0:D, :].bitcast(F32), 0.0).then_inc(zeroed, 1)
                dve.wait_ge(zeroed, b + 1)
                nc.vector.memset(k_l1[b][1][0:1, :].bitcast(F32), 1.0)

            def layernorm_stats(base):
                for j in range(TOK):
                    if base == 0 and j % 4 == 0:
                        dve.wait_ge(x_in[j // 4], 16)
                    nc.vector.bn_stats(st[:, j, :], xacc[:, j, :]).then_inc(ln_stats, 1)
                for j in range(TOK):
                    dve.wait_ge(ln_stats, base + j + 1)
                    nc.vector.bn_aggr(mv[:, j, :], st[:, j, :]).then_inc(stats, 1)

            def layernorm(base, n):
                dve.wait_ge(sd_ready, n)
                nc.vector.reciprocal(rs[:, :], sd[:, :]).then_inc(rs_ready, 1)
                dve.wait_ge(rs_ready, n)
                for j in range(TOK):
                    nc.vector.tensor_scalar(xn[:, j, :], xacc[:, j, :], mv[:, j, 0:1], rs[:, j:j + 1],
                                            ALU.subtract, ALU.mult).then_inc(xn_ready, 1)

            layernorm_stats(0)
            layernorm(0, 1)

            def take_turned(n, dst, cols, extra=None):
                dve.wait_ge(turned, n + 1)
                last = nc.vector.tensor_copy(dst, quad[n % 4][:, 0:cols])
                if extra is not None:
                    last = nc.vector.tensor_copy(extra, quad[n % 4][:, cols - 1:cols])
                last.then_inc(took_dve, 1)

            for n in range(1, 16, 2):
                take_turned(n, *turned_to(n))

            def unit_max(g, n, deep):
                bank = mring[n % 6] if deep else mring[n % 2]
                h, j, u = n // (UNITS // 2), n % (UNITS // 2) // 4, n % 4
                dve.wait_ge(max_full, g * UNITS + (n + 1))
                nc.vector.tensor_reduce(mx[:, h, j, u:u + 1], bank[:, 0:MPIECES[u][1]], AX.X, ALU.max)\
                  .then_inc(max_free, 1)
                if n == UNITS - 1:
                    dve.wait_ge(max_free, g * UNITS + UNITS)
                    nc.vector.tensor_reduce(nm[:, :], mx[:, :, :, :].rearrange("p h j u -> p (h j) u"), AX.X,
                                            ALU.max, negate=True).then_inc(nm_ready, 1)

            def add(p, i):
                t, rows = i % TT, key_tile(i % TT)
                if t == 0:
                    return
                acc = psum_p[0:rows, 0:SPLIT]
                dve.wait_ge(exp_done, p * STEPS + (i + 1))
                if t == 1:
                    if not (isinstance(p, int) and p == 0 and i < TT):
                        dve.wait_ge(desk_full, desk_before(p, "D3'" if i < TT else f"D{i // TT - 1}") + 1)
                    nc.vector.tensor_tensor(acc, ring[:, (i - 1) % RING, 0:SPLIT], ring[:, i % RING, 0:SPLIT],
                                            ALU.add).then_inc(add_a, 2)
                else:
                    dve.wait_ge(add_a, p * STEPS + i)
                    nc.vector.tensor_tensor(acc, acc, ring[0:rows, i % RING, 0:SPLIT], ALU.add)\
                      .then_inc(add_a, 1)

            def desk_piece(p, name, b):
                k = name[0]
                if k == "O":
                    c, u = int(name[2]), "ab".index(name[1])
                    dve.wait_ge(desk_full, desk_before(p, name) + 1)
                    dst = xacc[:, 4 * c + 2 * u:4 * c + 2 * u + 2, :]
                    nc.vector.scalar_tensor_tensor(out=dst, in0=desk[:, :].rearrange("p (a m) -> p a m", m=M),
                                                   scalar=tg[:, 0:1], in1=dst, op0=ALU.mult, op1=ALU.add)\
                      .then_inc(desk_free, 1)

            def normalise(done, q, p, name):
                cols = slice(q * P, (q + 1) * P)
                half = name[1]
                if q == 0:
                    dve.wait_ge(desk_free, desk_before(p, name) + 1)
                    dve.wait_ge(o_copied, done + 1)
                nc.vector.reciprocal(rden[:, cols], rden[:, cols]).then_inc(den_inv, 1)
                dve.wait_ge(den_inv, done * 4 + (q + 1))
                o = o_sb[:, int(half) % 2, cols]
                nc.vector.tensor_tensor(o, o, rden[:, cols], ALU.mult).then_inc(o_ready, 1)

            for n in range(UNITS):
                unit_max(0, n, True)

            def window(p, b, first=False, last=False):
                for i in range(STEPS):
                    c, t = i // TT, i % TT
                    units = [] if last and c == CHUNKS - 1 else units_at(i)
                    for n in units[:2]:
                        unit_max(p * CHUNKS + (c + 1), n, False)
                    if i:
                        add(p, i - 1)
                    if t in QUARTERS and not (first and c == 0):
                        normalise(p * CHUNKS + (c - 1), QUARTERS[t], p, "D3'" if c == 0 else f"D{c - 1}")
                    for n in units[2:]:
                        unit_max(p * CHUNKS + (c + 1), n, False)
                    name = at_step(i, first, last)
                    if name:
                        desk_piece(p, name, 1 - b)
                add(p, STEPS - 1)

            dve.wait_ge(tg_ready, 1)
            window(0, 0, first=True)
            with dve.Fori(0, PAIRS // 2 - 1) as n:
                window(1 + 2 * n, 1)
                window(2 + 2 * n, 0)
            window(PAIRS - 1, 1, last=True)
            for q in range(4):
                normalise(PAIRS * CHUNKS - 1, q, PAIRS, "D3'")
            for name in OUT3:
                desk_piece(PAIRS, name, 0)

            dve.wait_ge(desk_free, desk_before(PAIRS, "Ob3'") + 1)
            layernorm_stats(TOK)
            layernorm(TOK, 2)

            def lane_maxima(n, it, src, axis=AX.X):
                nc.vector.tensor_reduce(lanes[:, n, it:it + 1], src, axis, ALU.max,
                                        apply_absolute_value=True).then_inc(lane_max, 1)

            def global_scale(n, tiles):
                dve.wait_ge(lane_max, {X: 4, GATE: 10, UP: 22, GS: 22, OUT: 28}[n])
                nc.vector.tensor_reduce(part[:, n:n + 1], lanes[:, n, 0:tiles], AX.X, ALU.max).then_inc(gm_part, 1)
                if n == GS:
                    nc.vector.tensor_scalar(unit[:, n:n + 1], sc1[:, GATE, 0:1], 1.0 / SIG, None, ALU.mult)\
                      .then_inc(gm_step, 1)
                elif n == OUT:
                    nc.vector.tensor_tensor(unit[:, n:n + 1], sc1[:, UP, 0:1], sc1[:, GS, 0:1], ALU.mult)\
                      .then_inc(gm_step, 1)
                else:
                    nc.vector.memset(unit[:, n:n + 1], 1.0).then_inc(gm_step, 1)
                dve.wait_ge(gm_row, n + 1)
                nc.vector.tensor_reduce(big[:, n:n + 1], mb[0:1, 0:P], AX.X, ALU.max).then_inc(gm_step, 1)
                dve.wait_ge(gm_step, 6 * n + 2)
                nc.vector.tensor_scalar(raw[:, n:n + 1], big[:, n:n + 1], unit[:, n:n + 1], 1.0 / QMAX,
                                        ALU.mult, ALU.mult).then_inc(gm_step, 1)
                dve.wait_ge(gm_step, 6 * n + 3)
                nc.vector.tensor_scalar(sc1[:, n, 0:1], raw[:, n:n + 1], TINY, None, ALU.max).then_inc(gm_step, 1)
                dve.wait_ge(gm_step, 6 * n + 4)
                nc.vector.reciprocal(inv[:, n:n + 1], sc1[:, n, 0:1]).then_inc(gm_step, 1)
                dve.wait_ge(gm_step, 6 * n + 5)
                nc.vector.tensor_tensor(sc1[:, n, 1:2], inv[:, n:n + 1], unit[:, n:n + 1], ALU.mult)\
                  .then_inc(gm_step, 1)
                dve.wait_ge(gm_bc, n + 1)
                nc.vector.tensor_copy(scb[:, n, :], mb[:, CHUNK:CHUNK + 2]).then_inc(gm_ready, 1)
                dve.wait_ge(gm_ready, n + 1)

            dve.wait_ge(xn_ready, 2 * TOK)
            for c in range(4):
                lane_maxima(X, c, xn[:, 4 * c:4 * c + 4, :], AX.XY)
            global_scale(X, 4)
            for c in range(4):
                xc = xn[:, 4 * c:4 * c + 4, :]
                nc.vector.tensor_scalar(xc, xc, scb[:, X, 1:2], ROUND, ALU.mult, ALU.add).then_inc(x_rnd, 1)
            for c in range(4):
                xc = xn[:, 4 * c:4 * c + 4, :]
                dve.wait_ge(x_rnd, c + 1)
                nc.vector.tensor_scalar(xc, xc, ROUND, scb[:, X, 0:1], ALU.subtract, ALU.mult)\
                  .then_inc(xq_ready, 1)

            wb = w_nat[:, :, :].rearrange("p a (k i) -> p (a k) i", i=BLOCK)
            per_block = [P, 3 * FT * M // BLOCK, BLOCK]
            dve.wait_ge(wf_in, 48)
            nc.vector.tensor_reduce(wmax[:, :], wb, AX.X, ALU.max, apply_absolute_value=True).then_inc(w_step, 1)
            dve.wait_ge(w_step, 1)
            nc.vector.tensor_scalar(wsc[:, :], wmax[:, :], 1.0 / WMAX, TINY, ALU.mult, ALU.max).then_inc(w_step, 1)
            dve.wait_ge(w_step, 2)
            nc.vector.reciprocal(winv[:, :], wsc[:, :]).then_inc(w_step, 1)
            dve.wait_ge(w_step, 3)
            nc.vector.tensor_tensor(wb, wb, winv[:, :].unsqueeze(2).broadcast_to(per_block), ALU.mult)\
              .then_inc(w_step, 1)
            dve.wait_ge(w_step, 4)
            nc.vector.tensor_scalar(wb, wb, ROUND, ROUND, ALU.add, ALU.subtract).then_inc(w_step, 1)
            dve.wait_ge(w_step, 5)
            nc.vector.tensor_tensor(wb, wb, wsc[:, :].unsqueeze(2).broadcast_to(per_block), ALU.mult)\
              .then_inc(w_step, 1)
            for n in range(17, N_TURNED, 2):
                take_turned(n, *turned_to(n))

            for it in range(FT):
                dve.wait_ge(fg_free, 4 * (it + 1))
                lane_maxima(GATE, it, gate[:, it, :])
            global_scale(GATE, FT)
            for it in range(FT):
                nc.vector.tensor_scalar(gate[:, it, :], gate[:, it, :], scb[:, GATE, 1:2], ROUND,
                                        ALU.mult, ALU.add).then_inc(g_rnd, 1)
            for it in range(FT):
                sg = sig[it % 2][:, :]
                dve.wait_ge(sg_ready, it + 1)
                nc.vector.tensor_scalar(sg, sg, SIG, ROUND, ALU.mult, ALU.add).then_inc(s_rnd, 1)
                dve.wait_ge(s_rnd, it + 1)
                nc.vector.tensor_scalar(sg, sg, ROUND, SIG - 1, ALU.subtract, ALU.min).then_inc(s_int, 1)
                dve.wait_ge(fg_free, 4 * FT + 4 * (it + 1))
                lane_maxima(UP, it, up[:, it, :])
                dve.wait_ge(s_int, it + 1)
                nc.vector.tensor_tensor(gate[:, it, :], gate[:, it, :], sg, ALU.mult).then_inc(gs_ready, 1)
                dve.wait_ge(gs_ready, it + 1)
                lane_maxima(GS, it, gate[:, it, :])
            global_scale(UP, FT)
            global_scale(GS, FT)
            for it in range(FT):
                g = gate[:, it, :]
                nc.vector.tensor_scalar(g, g, scb[:, GS, 1:2], ROUND, ALU.mult, ALU.add).then_inc(gs_rnd, 1)
                dve.wait_ge(gs_rnd, it + 1)
                nc.vector.tensor_scalar(g, g, ROUND, None, ALU.subtract).then_inc(gs_int, 1)
                dve.wait_ge(gs_int, it + 1)
                dve.wait_ge(u_rnd, it + 1)
                nc.vector.scalar_tensor_tensor(out=g, in0=up[:, it, :], scalar=ROUND, in1=g,
                                               op0=ALU.subtract, op1=ALU.mult).then_inc(o_prod, 1)
                dve.wait_ge(o_prod, it + 1)
                lane_maxima(OUT, it, g)
            global_scale(OUT, FT)
            for it in range(FT):
                g = gate[:, it, :]
                dve.wait_ge(o_rnd, it + 1)
                nc.vector.tensor_scalar(g, g, ROUND, scb[:, OUT, 0:1], ALU.subtract, ALU.mult)\
                  .then_inc(o_quant, 1)
            for j in range(TOK):
                dve.wait_ge(dn_full, j + 1)
                nc.vector.scalar_tensor_tensor(out=xacc[:, j, :], in0=quad[j % 4][:, 0:M], scalar=tg[:, 1:2],
                                               in1=xacc[:, j, :], op0=ALU.mult, op1=ALU.add).then_inc(dn_free, 1)

        @block.tensor
        def _(pe):
            def mm(out_, lhsT, rhs, start=True, stop=True):
                return nc.tensor.matmul(out_, lhsT, rhs, start=start, stop=stop)

            def turn(n):
                src, ready, value = turned_from(n)
                pe.wait_ge(ready, value)
                if n >= 4:
                    pe.wait_ge(took_act if n % 2 == 0 else took_dve, (n - 4) // 2 + 1)
                at = 0
                for ap, rows in src:
                    last = nc.tensor.transpose(quad[n % 4][:, at:at + rows], ap, ident[0:rows, 0:rows])
                    at += rows
                last.then_inc(turned, 1)

            def desk_piece(p, name, b):
                k = name[0]
                n = int(name[1]) if k in "QKVTD" else 0
                if name == "Q0":
                    pe.wait_ge(w_in, (p + 1) * 96 + 96)
                if k == "D":
                    done = p * STEPS + (0 if name.endswith("'") else TT * (n + 1))
                    pe.wait_ge(add_a, done)
                    pe.wait_ge(add_b, done)
                if k == "O":
                    n = int(name[2])
                    prev = name.endswith("'")
                    pe.wait_ge(o_ready, (p - 1 if prev else p) * (4 * CHUNKS) + (4 * n + 2 + 2 * "ab".index(name[1])))
                    if not prev:
                        pe.wait_ge(wo_in, p * 16 + 16)
                if k == "T":
                    pe.wait_ge(nm_ready, p * CHUNKS + ((n or CHUNKS) + 1))
                if not (isinstance(p, int) and p == -1 and name == "Q0"):
                    pe.wait_ge(desk_free, desk_before(p, name))
                if k in "QK":
                    src, w = (xnT, w_qkv[0]) if k == "Q" else (ctxT, w_qkv[1])
                    c0, cols = (n * CHUNK, CHUNK) if k == "Q" else k_cols(n)
                    for kt in range(KT):
                        last = mm(desk[:, 0:cols], w[:, kt, :], src[:, kt, c0:c0 + cols], kt == 0, kt == KT - 1)
                if k == "V":
                    for t in range(4 * n, min(4 * n + 4, TT)):
                        rows = key_tile(t)
                        for kt in range(KT):
                            last = mm(desk[0:rows, (t % 4) * P:(t % 4 + 1) * P], ctxT[:, kt, t * P:t * P + rows],
                                      w_qkv[2][:, kt, :], kt == 0, kt == KT - 1)
                if k == "T":
                    last = nc.tensor.transpose(desk[0:2 * TOK // CHUNKS, 0:P], nm[:, :], ident[:, :])
                if k == "D":
                    for h in range(2):
                        last = mm(desk[h * D:(h + 1) * D, :], ones[:, :], psum_p[:, h * CHUNK:(h + 1) * CHUNK])
                if k == "O":
                    for j in range(2):
                        tok = (2 * "ab".index(name[1]) + j) * P
                        last = mm(desk[:, j * M:(j + 1) * M], o_sb[:, n % 2, tok:tok + P], w_o[:, :])
                last.then_inc(desk_full, 1)

            def unit_scores(q, c, n, b, deep):
                bank = mring[n % 6] if deep else mring[n % 2]
                h, j, u = n // (UNITS // 2), c * 4 + n % (UNITS // 2) // 4, n % 4
                if c == 0 and n == 0:
                    pe.wait_ge(lo_ready, q * 16 + 16)
                if deep and n >= 6:
                    pe.wait_ge(max_free, n - 5)
                if not deep:
                    pe.wait_ge(max_free, q * (CHUNKS * UNITS) + (c * UNITS + n - 1))
                k0, w = MPIECES[u]
                mm(bank[:, 0:w], q_hl[b][h][:, j * P:(j + 1) * P], k_hh[b][h][:, k0:k0 + w])\
                    .then_inc(max_full, 1)

            def scores(p, i, b, between):
                c, t = i // TT, i % TT
                rows = key_tile(t)
                if t == 0:
                    pe.wait_ge(shift_in, p * (32 * CHUNKS) + 32 * (c + 1))
                if isinstance(p, int) and p == 0 and i < 2:
                    pe.wait_ge(max_free, UNITS)
                else:
                    pe.wait_ge(exp_done, p * STEPS + (i - 1))
                qs = slice(c * CHUNK, (c + 1) * CHUNK)
                for h in range(2):
                    dst = sc[i % 2][0:rows, h * CHUNK:(h + 1) * CHUNK]
                    deep = D + 1 if h == 0 else P
                    mm(dst, k_hh[b][h][:, t * P:t * P + rows], q_hl[b][h][:, qs], True, False)
                    last = mm(dst, k_l1[b][h][0:deep, t * P:t * P + rows], q_hm[b][h][0:deep, qs], False, True)
                    if h == 0:
                        between()
                last.then_inc(sc_full, 1)

            def values(p, i, b):
                c, t = i // TT, i % TT
                rows = key_tile(t)
                pe.wait_ge(exp_done, p * STEPS + (i + 1))
                if t == 0 and not (isinstance(p, int) and p == 0 and c == 0):
                    pe.wait_ge(o_copied, p * CHUNKS + c)
                for h in range(2):
                    last = mm(ob[h * D:(h + 1) * D, :], v_pair[b][0:rows, t, h * D:(h + 1) * D],
                              ring[0:rows, i % RING, h * CHUNK:(h + 1) * CHUNK], t == 0, t == TT - 1)
                last.then_inc(pv_done, 1)

            def window(p, b, first=False, last=False):
                for i in range(STEPS):
                    c = i // TT
                    units = [] if last and c == CHUNKS - 1 else units_at(i)
                    ahead = (p, c + 1) if c < CHUNKS - 1 else (p + 1, 0)
                    ub = b if c < CHUNKS - 1 else 1 - b

                    def between():
                        for n in units[:1]:
                            unit_scores(*ahead, n, ub, False)

                    scores(p, i, b, between)
                    for n in units[1:2]:
                        unit_scores(*ahead, n, ub, False)
                    name = at_step(i, first, last)
                    if name:
                        desk_piece(p, name, 1 - b)
                    for n in units[2:4]:
                        unit_scores(*ahead, n, ub, False)
                    if i:
                        values(p, i - 1, b)
                    for n in units[4:]:
                        unit_scores(*ahead, n, ub, False)
                values(p, STEPS - 1, b)

            pe.wait_ge(consts, 1)
            for n in range(16):
                turn(n)
            pe.wait_ge(took_act, 8)
            pe.wait_ge(took_dve, 8)
            for name in PREP:
                desk_piece(-1, name, 0)
            for n in range(UNITS):
                unit_scores(0, 0, n, 0, True)
            desk_piece(-1, "T0", 0)
            window(0, 0, first=True)
            with pe.Fori(0, PAIRS // 2 - 1) as n:
                window(1 + 2 * n, 1)
                window(2 + 2 * n, 0)
            window(PAIRS - 1, 1, last=True)
            for name in OUT3:
                desk_piece(PAIRS, name, 0)

            def find_scale(n):
                pe.wait_ge(gm_part, n + 1)
                mm(mb[0:1, 0:P], part[:, n:n + 1], ident[:, :]).then_inc(gm_row, 1)
                pe.wait_ge(gm_step, 6 * n + 6)
                mm(mb[:, CHUNK:CHUNK + 2], ones1[0:1, :], sc1[0:1, n, :]).then_inc(gm_bc, 1)

            find_scale(X)
            for n in range(16, N_TURNED):
                turn(n)
            pe.wait_ge(took_act, (N_TURNED + 1) // 2)
            pe.wait_ge(took_dve, N_TURNED // 2)

            def product(n):
                m, it, c = n // (4 * FT), n % (4 * FT) // 4, n % 4
                if n >= 4:
                    pe.wait_ge(fg_free, n - 3)
                for kt in range(KT):
                    last = mm(quad[n % 4], wg_up[:, m, kt, it * P:(it + 1) * P],
                              xqT[:, kt, c * CHUNK:(c + 1) * CHUNK], kt == 0, kt == KT - 1)
                last.then_inc(fg_full, 1)

            for n in range(8 * FT):
                product(n)
                if n == 4 * FT + 2:
                    find_scale(GATE)
            for n in (UP, GS, OUT):
                find_scale(n)
            pe.wait_ge(fg_free, 8 * FT)
            for j in range(TOK):
                if j >= 4:
                    pe.wait_ge(dn_free, j - 3)
                for it in range(FT):
                    if j == 0:
                        pe.wait_ge(o_quant, it + 1)
                    last = mm(quad[j % 4][:, 0:M], gate[:, it, j * P:(j + 1) * P], w_dn[:, it, :],
                              it == 0, it == FT - 1)
                last.then_inc(dn_full, 1)


_INS = ["x", "ctx_1024", "g_xattn", "g_ffn", "L0_xattn_Wq", "L0_xattn_Wk", "L0_xattn_Wv", "L0_xattn_Wo",
        "L0_ffn_w_gate", "L0_ffn_w_up", "L0_ffn_w_down"]


def kernel(**inputs):
    import numpy as np
    import concourse.bacc as bacc
    from concourse.bass_utils import run_bass_kernel_spmd as run

    nc = bacc.Bacc("TRN2", target_bir_lowering=False, num_devices=1)
    arrays, args = {}, []
    for name in _INS:
        a = np.ascontiguousarray(inputs[name])
        arrays[f"in_{name}"] = a
        args.append(nc.dram_tensor(f"in_{name}", a.shape, mybir.dt.from_np(a.dtype), kind="ExternalInput").ap())
    args.append(nc.dram_tensor("out_0", (1, S, M), F32, kind="ExternalOutput").ap())
    gated_block(nc, *args)
    r = run(nc, [arrays], core_ids=[0])
    return r.results[0]["out_0"]
```

```python
import concourse.bass as bass
from concourse import mybir
from contextlib import ExitStack
import numpy as np

F32 = mybir.dt.float32
F32R = mybir.dt.float32r
I16 = mybir.dt.int16
I32 = mybir.dt.int32
ALU = mybir.AluOpType
ACT = mybir.ActivationFunctionType
AX = mybir.AxisListType

S = 2048
T = 1601
M = 256
H = 16
D = 64
F = 768
BLOCK = 32
P = 128

KT = M // P
FT = F // P
PAIRS = H // 2
CHUNK = 512
CHUNKS = S // CHUNK
TOK = S // P
TT = -(-T // P)
TLAST = T - (TT - 1) * P
TE = T + 1
STEPS = CHUNKS * TT
HALF = 400
MPIECES = [(0, HALF), (HALF, HALF), (2 * HALF, HALF + 2), (TE - HALF - 2, HALF + 2)]
UNITS = 2 * (TOK // CHUNKS) * len(MPIECES)
RING = 4
SPLIT = 256
SCALE = float(D) ** -0.5
EPS = 1e-5
ROUND = 1.5 * 2.0 ** 23
QMAX = 2.0 ** 15 - 1
WMAX = 2.0 ** 3 - 1
TINY = 1e-12
SIG = 65536.0

N_TURNED = 24
ACT_TURNED = [0, 2, 4, 6, 8]
DVE_TURNED = [n for n in range(N_TURNED) if n not in ACT_TURNED]
N_WT = 8
N_DN = 3
W_STEPS = 12
WEIGHTS_AT = [i for i in range(1, STEPS) if i % TT not in (2, 9)][:2 * W_STEPS]
TURNED_AT = [41, 42, 43, 45, 46, 47, 49, 50]
LAYERNORM_AT = [36, 37, 40, 44, 48, 50]
ACT_ROUNDS = [0, 1, 3, 4]
POOL_TILES = [1, 3]
DVE_UP = [0, 2, 4]
DVE_TILES = [it for it in range(FT) if it not in POOL_TILES]
X, GATE, UP, GS, OUT = range(5)

OUT3 = ["D3'", "Oa3'", "Ob3'"]
PREP = [f"{k}{n}" for k in "KQV" for n in range(4)]
BEFORE_M = ["K0", "K1", "K2", "K3", "Q0"]
WITHIN_M = {5: "Q1", 11: "V0", 17: "V1", 23: "V2", 29: "V3"}
PROLOGUE = BEFORE_M + [WITHIN_M[n] for n in sorted(WITHIN_M)] + ["T0"]
D_AT, OA_AT, OB_AT, T_AT, PREP_AT = 1, 5, 9, 11, (2, 8, 12)
FULL = {}
for _c in range(CHUNKS):
    _d = "3'" if _c == 0 else str(_c - 1)
    FULL.update({TT * _c + _i: _n for _i, _n in (
        (D_AT, "D" + _d), (OA_AT, "Oa" + _d), (OB_AT, "Ob" + _d), (T_AT, f"T{(_c + 1) % CHUNKS}"),
        *((PREP_AT[_k], PREP[3 * _c + _k]) for _k in range(3)))})
FIRST = {i: n for i, n in FULL.items() if n != "Ob3'"}
FIRST.update(dict(zip(sorted((D_AT, PREP_AT[0], OA_AT)), ("Q2+", "Q3+", "K0"))))
LAST = {i: n for i, n in FULL.items() if n not in PREP + ["T0"]}
LAST.update({i: f"W{n}" for n, i in enumerate(TURNED_AT)})
assert len(LAST) == 4 * CHUNKS - 1 + N_WT
UNITS_AT = [2, 4, 4, 0, 1, 3, 2, 2, 4, 3, 2, 2, 3]
UNITS_LAST_AT = [3, 4, 3, 0, 2, 2, 2, 1, 4, 4, 2, 2, 3]
LEAD = 2
AHEAD = (2, 6, 2)
EARLY = sum(UNITS_AT[-LEAD:])
QUARTERS = {2: 0, 3: 1, 4: 2, 7: 3}


def desk_order(first=False, last=False):
    return FIRST if first else LAST if last else FULL


def desk_before(p, name):
    def at(order):
        return [order[i] for i in sorted(order)].index(name)
    if isinstance(p, int) and p == -1:
        return PROLOGUE.index(name)
    if isinstance(p, int) and p == 0:
        return len(PROLOGUE) + at(FIRST)
    ahead = len(PROLOGUE) + len(FIRST) - len(FULL)
    if isinstance(p, int) and p == PAIRS:
        return ahead + len(FULL) * (PAIRS - 1) + len(LAST) + OUT3.index(name)
    return p * len(FULL) + (ahead + at(LAST if isinstance(p, int) and p == PAIRS - 1 else FULL))


def prepared(p, name, b):
    return (p, 1 - b) if name.endswith("+") else (p + 1, b)


def units_at(i, last=False):
    c, t = i // TT, i % TT
    table = UNITS_LAST_AT if last else UNITS_AT
    if t < TT - LEAD:
        chunk, done = c + 1, EARLY + sum(table[:t])
    else:
        chunk, done = c + 2, sum(table[TT - LEAD:t])
    if last and chunk >= CHUNKS:
        return [], chunk
    return list(range(done, done + table[t])), chunk


def ug_made(it):
    return 2 * (it + 1) - sum(1 for t in DVE_UP if t <= it)


assert sum(UNITS_AT) == sum(UNITS_LAST_AT) == UNITS and sum(UNITS_LAST_AT[-LEAD:]) == EARLY


def gated_block(nc, x, ctx, g_xattn, g_ffn, wq, wk, wv, wo, w_gate, w_up, w_down, out):
    whole = ExitStack()
    with whole:
        def sem(name):
            return whole.enter_context(nc.semaphore(name))

        def keep(name, shape, dt=F32):
            return whole.enter_context(nc.sbuf_tensor(name, shape, dt))

        xacc = keep("xacc", [P, TOK, M])
        ident = keep("ident", [P, P])
        ones = keep("ones", [P, D])
        gates = keep("gates", [P, 2])
        tg = keep("tg", [P, 2])
        st = keep("st", [P, TOK, 6])
        mv = keep("mv", [P, TOK, 2])
        sd = keep("sd", [P, TOK])
        rs = keep("rs", [P, TOK])
        epst = keep("epst", [P, 1])
        ones1 = keep("ones1", [1, P])
        hi_x = keep("hi_x", [P, TOK])
        lo_x = keep("lo_x", [P, TOK])
        rsi = keep("rsi", [P, TOK])
        tgs = keep("tgs", [P, 1])
        lanes = keep("lanes", [P, 5, 6])
        part = keep("part", [P, 5])
        big = keep("big", [1, 5])
        unit = keep("unit", [1, 5])
        raw = keep("raw", [1, 5])
        inv = keep("inv", [1, 5])
        sc1 = keep("sc1", [1, 5, 2])
        scb = keep("scb", [P, 5, 2])
        ring = keep("ring", [P, RING, 2 * CHUNK])
        xn = ring[:, :, :].rearrange("p r (a m) -> p (r a) m", m=M)

        att = ExitStack()

        def sb(name, shape, dt=F32):
            return att.enter_context(nc.sbuf_tensor(name, shape, dt))

        q_hl, q_hm, k_hh, k_l1, v_pair = [], [], [], [], []
        for b in range(2):
            q_hl.append([sb(f"q_hl{b}{h}", [P, S], F32R) for h in range(2)])
            q_hm.append([sb(f"q_hm{b}{h}", [P, S], F32R) for h in range(2)])
            k_hh.append([sb(f"k_hh{b}{h}", [P, TE], F32R) for h in range(2)])
            k_l1.append([sb(f"k_l1{b}{h}", [P, TE], F32R) for h in range(2)])
            v_pair.append(sb(f"v_pair{b}", [P, TT, P]))
        ctx_nat = [v_pair[b][:, :, :] for b in range(2)]
        xnT = sb("xnT", [P, KT, S])
        ctxT = sb("ctxT", [P, KT, TE])
        psum_p = sb("psum_p", [P, 2 * CHUNK])
        o_sb = sb("o_sb", [P, 2, CHUNK])
        rden = sb("rden", [P, CHUNK])
        stage = sb("stage", [P, CHUNK])
        w_qkv = [sb(f"w_{n}", [P, KT, P]) for n in "qkv"]
        w_o = sb("w_o", [P, M])
        mx = sb("mx", [P, 2, TOK // CHUNKS, len(MPIECES)])
        nm = sb("nm", [P, 2 * TOK // CHUNKS])
        nmT = sb("nmT", [2 * TOK // CHUNKS, P], F32R)
        att.close()

        ffn = ExitStack()

        def sf(name, shape, dt=F32):
            return ffn.enter_context(nc.sbuf_tensor(name, shape, dt))

        def one_after_the_other(first, *then):
            with ExitStack() as scope:
                buffer = scope.enter_context(nc.sbuf_tensor(*first))
            others = [sf(*t) for t in then]
            size = [sum(4 // (2 if dt == I16 else 1) * int(np.prod(shape[1:])) for _, shape, dt in ts)
                    for ts in ((first,), then)]
            if size[0] > size[1]:
                sf(first[0] + "_rest", [P, (size[0] - size[1]) // 4])
            return buffer, others

        w_nat, (xq_lo,) = one_after_the_other(("w_nat", [P, 2 * FT, M], F32), ("xq_lo", [P, KT, S], F32R))
        wmax = sf("wmax", [P, 3 * FT * M // BLOCK])
        wsc = sf("wsc", [P, 3 * FT * M // BLOCK])
        winv = sf("winv", [P, 3 * FT * M // BLOCK])
        w_hl, ints = one_after_the_other(("w_hl", [P, 2, 2, KT, F], F32R),
                                         *((f"ints{n}", [P, S], I16) for n in range(4)))
        w_hi, w_lo = w_hl[:, :, 0], w_hl[:, :, 1]
        w_dn = sf("w_dn", [P, FT, M])
        gate = sf("gate", [P, FT, S])
        up = sf("up", [P, FT, S])
        wd_nat = sf("wd_nat", [P, FT, M])
        xq_hi = sf("xq_hi", [P, KT, S], F32R)
        ffn.close()
        xn2 = up[:, FT - 2:, :].rearrange("p a s -> p (a s)").rearrange("p (j m) -> p j m", m=M)
        int_a, int_b = ([ints[2 * m + b][:, :] for b in range(2)] for m in range(2))
        sig = [ring[:, 2 * b:2 * b + 2, :].rearrange("p r n -> p (r n)") for b in range(2)]
        int_s = [s_.bitcast(I32) for s_ in sig]

        sc = [whole.enter_context(nc.psum_tensor(f"scores{b}", [P, 2 * CHUNK], F32)) for b in range(2)]
        mb = whole.enter_context(nc.psum_tensor("mb", [P, 2 * CHUNK], F32))
        ob = whole.enter_context(nc.psum_tensor("ob", [P, CHUNK], F32))
        desk = whole.enter_context(nc.psum_tensor("desk", [P, CHUNK], F32))
        quad = [sc[n // 2][:, (n % 2) * CHUNK:(n % 2 + 1) * CHUNK] for n in range(4)]
        mring = [mb[:, 0:CHUNK], mb[:, CHUNK:]] + quad

        x_in = [sem(f"x_in{c}") for c in range(4)]
        ctx_in, g_in = [sem(f"ctx_in{b}") for b in range(KT)], sem("g_in")
        wq_in, wk_in, wv_in = sem("wq_in"), sem("wk_in"), sem("wv_in")
        wo_in, shift_in = sem("wo_in"), sem("shift_in")
        consts, ident0 = sem("consts"), sem("ident0")
        stats, sd_ready, rs_ready, xn_ready = sem("stats"), sem("sd_ready"), sem("rs_ready"), sem("xn_ready")
        tg_ready, table_in = sem("tg_ready"), sem("table_in")
        turned = sem("turned")
        took_act, took_dve = sem("took_act"), sem("took_dve")
        desk_full, desk_free = sem("desk_full"), sem("desk_free")
        hi_ready, lo_ready, zeroed = sem("hi_ready"), sem("lo_ready"), sem("zeroed")
        max_full, max_free, nm_ready = sem("max_full"), sem("max_free"), sem("nm_ready")
        sc_full, exp_done, pv_done = sem("sc_full"), sem("exp_done"), sem("pv_done")
        add_a, add_b, den_inv = sem("add_a"), sem("add_b"), sem("den_inv")
        o_copied, o_ready = sem("o_copied"), sem("o_ready")
        wf_in, w_step = [sem(f"wf_in{n}") for n in range(3)], sem("w_step")
        ln_stats = sem("ln_stats")
        lane_max = sem("lane_max")
        gm_part, gm_row, gm_step, gm_bc, gm_ready = (
            sem(f"gm_{n}") for n in ("part", "row", "step", "bc", "ready"))
        gm_unit = sem("gm_unit")
        x_range, x_dev, x_cen, xq_ready = sem("x_range"), sem("x_dev"), sem("x_cen"), sem("xq_ready")
        fg_full, fg_free = sem("fg_full"), sem("fg_free")
        g0_int, w_split, x_split = sem("g0_int"), sem("w_split"), sem("x_split")
        g_int, sg_ready, s_int, gs_ready = sem("g_int"), sem("sg_ready"), sem("s_int"), sem("gs_ready")
        u_int, ug_int, o_made, o_pool = sem("u_int"), sem("ug_int"), sem("o_made"), sem("o_pool")
        o_rnd, o_rnd2, o_quant = sem("o_rnd"), sem("o_rnd2"), sem("o_quant")
        wd_full, wd_free = sem("wd_full"), sem("wd_free")
        dn_full, dn_free, y_out = sem("dn_full"), sem("dn_free"), sem("y_out")

        wq_v, wk_v, wv_v = (w.rearrange("(a h) (c p) d -> a p c h d", h=2, p=P) for w in (wq, wk, wv))
        wo_v = wo.rearrange("(a p) n -> a p n", p=P)
        x_v = x[0].rearrange("(j p) m -> p j m", p=P)
        out_v = out[0].rearrange("(j p) m -> p j m", p=P)

        def turned_from(n):
            if n < 8:
                kt, c = n // 4, n % 4
                tiles = range(4 * c, min(4 * c + 4, TT))
                return [(ctx_nat[kt][0:key_tile(t), t, :], key_tile(t)) for t in tiles], ctx_in[kt], 32
            if n < 24:
                kt, c = n % 2, n % 8 // 2
                src = [((xn if n < 16 else xn2)[:, 4 * c + j, kt * P:(kt + 1) * P], P) for j in range(4)]
                return (src, xn_ready, 4 * c + 4) if n < 16 else (src, xq_ready, c + 1)

        def weights_from(n):
            if n < 8:
                base, kt, g = n // 4 * FT, n % 4 // 2, n % 2
                return [w_nat[:, base + 3 * g + j, kt * P:(kt + 1) * P] for j in range(3)], W_STEPS * (n // 4 + 1)
            outs = wd_nat[:, :, :].rearrange("p (o a) m -> p o (a m)", o=M // P)
            return [outs[:, o, k * P:(k + 1) * P]
                    for k in (2 * (n - N_WT), 2 * (n - N_WT) + 1) for o in range(M // P)], 3 * W_STEPS

        def turned_to(n):
            kt, c = (n // 4, n % 4) if n < 8 else (n % 2, n % 8 // 2)
            dst = ctxT if n < 8 else xnT if n < 16 else xq_hi
            if n < 8 and c == 3:
                return ctxT[:, kt, c * CHUNK:T], TLAST, ctxT[:, kt, T:TE]
            return dst[:, kt, c * CHUNK:(c + 1) * CHUNK], CHUNK

        def weights_to(n):
            if n < N_WT:
                return w_hi[:, n // 4, n % 4 // 2, 3 * P * (n % 2):3 * P * (n % 2 + 1)], 3 * P
            return w_dn[:, 2 * (n - N_WT):2 * (n - N_WT) + 2, :].rearrange("p a m -> p (a m)"), CHUNK

        def prologue_bank(name):
            return (desk, ob)[PROLOGUE.index(name) % 2]

        def prologue_stage(name):
            return (stage[:, :], o_sb[:, 0, :])[PREP.index(name) % 2]

        def result(j):
            return (quad + [mb[:, 0:CHUNK], mb[:, CHUNK:], ob[:, :], desk[:, :]])[j % 8][:, 0:M]

        def key_tile(t):
            return TLAST if t == TT - 1 else P

        def k_cols(c):
            return c * CHUNK, min(CHUNK, TE - c * CHUNK)

        block = whole.enter_context(nc.Block())

        @block.sync
        def _(sp):
            for b in range(KT):
                sp.dma_start(ctx_nat[b][:, 0:TT - 1, :],
                             ctx[0, 0:(TT - 1) * P, b * P:(b + 1) * P].rearrange("(j p) m -> p j m", p=P))\
                  .then_inc(ctx_in[b], 16)
                sp.dma_start(ctx_nat[b][0:TLAST, TT - 1, :], ctx[0, (TT - 1) * P:T, b * P:(b + 1) * P])\
                  .then_inc(ctx_in[b], 16)

            def load(k, q):
                n = "qkv".index(k)
                for h in range(2):
                    sp.dma_start(w_qkv[n][:, :, h * D:(h + 1) * D], (wq_v, wk_v, wv_v)[n][q, :, :, h, :])\
                      .then_inc((wq_in, wk_in, wv_in)[n], 16)

            def send_shift(p, c, b):
                sp.wait_ge(desk_free, desk_before(p, f"T{c}") + 1)
                for h in range(2):
                    row = slice(D, D + 1) if h == 0 else slice(0, 1)
                    sp.dma_start(q_hm[b][h][row, c * CHUNK:(c + 1) * CHUNK].bitcast(F32),
                                 nmT[4 * h:4 * h + 4, :].bitcast(F32)).then_inc(shift_in, 16)

            def window(p, b, first=False, last=False):
                if not last:
                    order = desk_order(first, last)
                    sp.wait_ge(desk_full, desk_before(p, order[min(order)]))
                    load("k", p + 1)
                    load("v", p + 1)
                    if first:
                        sp.wait_ge(desk_full, desk_before(p, "Q3+") + 1)
                    load("q", p + 1)
                else:
                    sp.wait_ge(pv_done, p * STEPS)
                    sp.dma_start(w_nat[:, 0:FT, :], w_gate.rearrange("(j p) m -> p j m", p=P)).then_inc(wf_in[0], 16)
                    sp.dma_start(w_nat[:, FT:2 * FT, :], w_up.rearrange("(j p) m -> p j m", p=P)).then_inc(wf_in[1], 16)
                if not first:
                    sp.wait_ge(desk_full, desk_before(p, "Ob3'") + 1)
                    sp.dma_start(w_o[:, :], wo_v[p]).then_inc(wo_in, 16)
                for c in range(1, CHUNKS):
                    send_shift(p, c, b)
                if not last:
                    send_shift(p, 0, 1 - b)

            load("k", 0)
            for c in range(4):
                sp.dma_start(xacc[:, 4 * c:4 * c + 4, :], x_v[:, 4 * c:4 * c + 4, :]).then_inc(x_in[c], 16)
            for k in "qv":
                load(k, 0)
            sp.dma_start(gates[:, 0:1], g_xattn.unsqueeze(0).broadcast_to([P, 1])).then_inc(g_in, 16)
            sp.dma_start(gates[:, 1:2], g_ffn.unsqueeze(0).broadcast_to([P, 1])).then_inc(g_in, 16)
            sp.dma_start(w_o[:, :], wo_v[0]).then_inc(wo_in, 16)
            send_shift(-1, 0, 0)
            window(0, 0, first=True)
            with sp.Fori(0, PAIRS // 2 - 1) as n:
                window(1 + 2 * n, 1)
                window(2 + 2 * n, 0)
            window(PAIRS - 1, 1, last=True)
            sp.wait_ge(desk_full, desk_before(PAIRS, "Ob3'") + 1)
            sp.dma_start(wd_nat[:, :, :].rearrange("p (o a) m -> p o (a m)", o=M // P),
                         w_down.rearrange("(o p) m -> p o m", p=P)).then_inc(wf_in[2], 16)
            for c in range(4):
                sp.wait_ge(dn_free, 4 * c + 4)
                sp.dma_start(out_v[:, 4 * c:4 * c + 4, :], xacc[:, 4 * c:4 * c + 4, :]).then_inc(y_out, 16)
            sp.wait_ge(y_out, 64)

        @block.gpsimd
        def _(pool):
            nc.gpsimd.memset(ident[:, :], 0.0).then_inc(ident0, 1)
            nc.gpsimd.memset(ones[:, :], 1.0).then_inc(ident0, 1)
            nc.gpsimd.memset(epst[:, :], EPS).then_inc(ident0, 1)
            nc.gpsimd.memset(unit[:, 0:1], 1.0).then_inc(ident0, 1)
            nc.gpsimd.memset(ones1[:, :], 1.0).then_inc(ident0, 1)
            pool.wait_ge(ident0, 5)
            nc.gpsimd.affine_select(out=ident[:, :], in_=ident[:, :], compare_op=ALU.not_equal, fill=1.0,
                                    base=0, pattern=[[-1, P]], channel_multiplier=1).then_inc(consts, 1)
            pool.wait_ge(consts, 1)

            def clear(b):
                for n, (what, value) in enumerate(((k_l1[b][0][D:D + 1, :], 1.0), (q_hm[b][1][0:D, :], 0.0),
                                                   (k_l1[b][1][0:D, :], 0.0), (k_l1[b][1][0:1, :], 1.0))):
                    nc.gpsimd.memset(what.bitcast(F32), value).then_inc(zeroed, 1)
                    pool.wait_ge(zeroed, 4 * b + n + 1)

            def add(p, i):
                t, rows = i % TT, key_tile(i % TT)
                if t == 0:
                    return
                acc = psum_p[0:rows, SPLIT:]
                pool.wait_ge(exp_done, p * STEPS + (i + 1))
                if t == 1:
                    if not (isinstance(p, int) and p == 0 and i < TT):
                        pool.wait_ge(desk_full, desk_before(p, "D3'" if i < TT else f"D{i // TT - 1}") + 1)
                    nc.gpsimd.tensor_tensor(acc, ring[:, (i - 1) % RING, SPLIT:], ring[:, i % RING, SPLIT:],
                                            ALU.add).then_inc(add_b, 2)
                else:
                    pool.wait_ge(add_b, p * STEPS + i)
                    nc.gpsimd.tensor_tensor(acc, acc, ring[0:rows, i % RING, SPLIT:], ALU.add)\
                      .then_inc(add_b, 1)

            def split_low(p, name, b):
                q, b = prepared(p, name, b)
                k, n = name[0], int(name[1])
                c0, w = (n * CHUNK, CHUNK) if k == "Q" else k_cols(n)
                cols = slice(c0, c0 + w)
                staged = prologue_stage(name) if isinstance(p, int) and p == -1 else stage
                pool.wait_ge(hi_ready, q * 8 + (PREP.index(name[:2]) + 1))
                for h in range(2):
                    own = slice(h * D, (h + 1) * D)
                    hi, lo = (q_hm, q_hl) if k == "Q" else (k_hh, k_l1)
                    nc.gpsimd.tensor_tensor(lo[b][h][own, cols], staged[own, 0:w],
                                            hi[b][h][own, cols].bitcast(F32), ALU.subtract).then_inc(lo_ready, 1)
                    pool.wait_ge(lo_ready, q * 16 + (2 * PREP.index(name[:2]) + h + 1))

            def window(p, b, first=False, last=False):
                for i in range(STEPS):
                    add(p, i)
                    name = desk_order(first, last).get(i)
                    if name and name[0] in "QK":
                        if i % TT:
                            pool.wait_ge(add_b, p * STEPS + (i + 1))
                        split_low(p, name, 1 - b)

            clear(0)
            for name in PROLOGUE:
                if name[0] in "QK":
                    split_low(-1, name, 0)
            clear(1)
            window(0, 0, first=True)
            with pool.Fori(0, PAIRS // 2 - 1) as n:
                window(1 + 2 * n, 1)
                window(2 + 2 * n, 0)
            window(PAIRS - 1, 1, last=True)

            for c in range(CHUNKS):
                xc = xn2[:, 4 * c:4 * c + 4, :]
                pool.wait_ge(x_cen, 4 * c + 4)
                nc.gpsimd.tensor_scalar(xc, xc, 1.0, ROUND, ALU.mult, ALU.add).then_inc(xq_ready, 1)
            for it in range(FT):
                pool.wait_ge(sg_ready, it + 1)
                nc.gpsimd.tensor_scalar(int_s[it % 2], sig[it % 2], SIG, 0.0, ALU.mult, ALU.add).then_inc(s_int, 1)
            for n, it in enumerate(POOL_TILES):
                pool.wait_ge(ug_int, ug_made(it))
                nc.gpsimd.tensor_scalar(up[:, it, :], int_a[it % 2], 1.0, 0.0, ALU.mult, ALU.add).then_inc(o_pool, 1)
                nc.gpsimd.tensor_scalar(gate[:, it, :], int_b[it % 2], 1.0, 0.0, ALU.mult, ALU.add).then_inc(o_pool, 1)
                pool.wait_ge(o_pool, 3 * n + 2)
                nc.gpsimd.tensor_tensor(gate[:, it, :], gate[:, it, :], up[:, it, :], ALU.mult).then_inc(o_pool, 1)

        @block.scalar
        def _(act):
            def take_turned(n, dst, cols, extra=None):
                act.wait_ge(turned, n + 1)
                last = nc.scalar.activation(dst, quad[n % 4][:, 0:cols], ACT.Copy)
                if extra is not None:
                    last = nc.scalar.activation(extra, quad[n % 4][:, cols - 1:cols], ACT.Copy)
                last.then_inc(took_act, 1)

            def desk_piece(p, name, b):
                k = name[0]
                n = int(name[1]) if k in "QKVT" else 0
                prologue = isinstance(p, int) and p == -1
                bank = prologue_bank(name) if prologue else desk
                if k in "QK":
                    q, to = prepared(p, name, b)
                    c0, w = (n * CHUNK, CHUNK) if k == "Q" else k_cols(n)
                    cols = slice(c0, c0 + w)
                    done = PREP.index(name[:2])
                    act.wait_ge(desk_full, desk_before(p, name) + 1)
                    staged = stage
                    if prologue:
                        staged = prologue_stage(name)
                        if done >= 2:
                            act.wait_ge(lo_ready, 2 * (done - 1))
                    else:
                        act.wait_ge(lo_ready, q * 16 + 2 * done)
                    nc.scalar.activation(staged[:, 0:w], bank[:, 0:w], ACT.Copy).then_inc(desk_free, 1)
                    act.wait_ge(desk_free, desk_before(p, name) + 1)
                    for h in range(2):
                        for dst, half in ((q_hm, h), (q_hl, 1 - h)) if k == "Q" else ((k_hh, 0), (k_hh, 1)):
                            last = nc.scalar.activation(dst[to][h][half * D:(half + 1) * D, cols],
                                                        staged[h * D:(h + 1) * D, 0:w], ACT.Copy)
                    last.then_inc(hi_ready, 1)
                if k == "W":
                    dst, w = weights_to(int(name[1:]))
                    act.wait_ge(desk_full, desk_before(p, name) + 1)
                    nc.scalar.activation(dst, desk[:, 0:w], ACT.Copy)\
                       .then_inc(w_split, 1)
                if k == "V":
                    act.wait_ge(desk_full, desk_before(p, name) + 1)
                    if n < 3:
                        nc.scalar.activation(v_pair[b][:, 4 * n:4 * n + 4, :],
                                             bank[:, :].rearrange("p (a d) -> p a d", d=P), ACT.Copy)\
                          .then_inc(desk_free, 1)
                    else:
                        nc.scalar.activation(v_pair[b][0:TLAST, TT - 1, :], bank[0:TLAST, 0:P], ACT.Copy)\
                          .then_inc(desk_free, 1)
                if k == "T":
                    act.wait_ge(desk_full, desk_before(p, name) + 1)
                    if not (isinstance(p, int) and p == -1):
                        act.wait_ge(shift_in, p * (32 * CHUNKS) + 32 * (n or CHUNKS))
                    nc.scalar.activation(nmT[:, :], bank[0:2 * TOK // CHUNKS, 0:P], ACT.Copy).then_inc(desk_free, 1)
                if k == "D":
                    c = int(name[1])
                    done = (p - 1 if name.endswith("'") else p) * CHUNKS + c
                    if not (isinstance(p, int) and p == 0 and c == 0):
                        act.wait_ge(o_ready, done * 4)
                    act.wait_ge(desk_full, desk_before(p, name) + 1)
                    nc.scalar.activation(rden[:, :], desk[:, :], ACT.Copy).then_inc(desk_free, 1)

            act.wait_ge(consts, 1)
            nc.scalar.activation(sd[:, 0:1], epst[:, :], ACT.Sqrt).then_inc(table_in, 1)
            for n in range(0, 8, 2):
                take_turned(n, *turned_to(n))
            for name in PROLOGUE:
                if name == "K2":
                    act.wait_ge(stats, TOK)
                    act.wait_ge(table_in, 1)
                    nc.scalar.activation(sd[:, :], mv[:, :, 1], ACT.Sqrt, bias=epst[:, :]).then_inc(sd_ready, 1)
                    act.wait_ge(g_in, 32)
                    nc.scalar.activation(tg[:, :], gates[:, :], ACT.Tanh).then_inc(tg_ready, 1)
                if name == "Q0":
                    take_turned(8, *turned_to(8))
                desk_piece(-1, name, 0)

            def exp(p, i):
                rows = key_tile(i % TT)
                act.wait_ge(sc_full, p * STEPS + (i + 1))
                if not (isinstance(p, int) and p == 0 and i < RING):
                    act.wait_ge(pv_done, p * STEPS + (i - RING + 1))
                    act.wait_ge(add_a, p * STEPS + (i - RING + 1))
                    act.wait_ge(add_b, p * STEPS + (i - RING + 1))
                nc.scalar.activation(ring[0:rows, i % RING, :], sc[i % 2][0:rows, :], ACT.Exp, scale=SCALE)\
                  .then_inc(exp_done, 1)

            def copy_o(p, c):
                act.wait_ge(pv_done, p * STEPS + TT * (c + 1))
                if c < 2:
                    if not (isinstance(p, int) and p == 0):
                        act.wait_ge(desk_full, desk_before(p - 1, "Ob2") + 1 if c == 0 else desk_before(p, "Ob3'") + 1)
                else:
                    act.wait_ge(desk_full, desk_before(p, f"Ob{c - 2}") + 1)
                nc.scalar.activation(o_sb[:, c % 2, :], ob[:, :], ACT.Copy).then_inc(o_copied, 1)

            def window(p, b, first=False, last=False):
                for i in range(STEPS):
                    exp(p, i)
                    name = desk_order(first, last).get(i)
                    if name:
                        desk_piece(p, name, 1 - b)
                    if i and i % TT == 0:
                        copy_o(p, i // TT - 1)
                copy_o(p, CHUNKS - 1)

            window(0, 0, first=True)
            with act.Fori(0, PAIRS // 2 - 1) as n:
                window(1 + 2 * n, 1)
                window(2 + 2 * n, 0)
            window(PAIRS - 1, 1, last=True)
            desk_piece(PAIRS, "D3'", 0)

            act.wait_ge(stats, 2 * TOK)
            nc.scalar.activation(sd[:, :], mv[:, :, 1], ACT.Sqrt, bias=epst[:, :]).then_inc(sd_ready, 1)
            for n in range(16, N_TURNED):
                dst, cols = turned_to(n)
                act.wait_ge(turned, n + 1)
                nc.scalar.activation(dst, quad[n % 4], ACT.Copy, bias=-ROUND).then_inc(x_split, 1)

            def take_product(n):
                dst, m = (gate, n) if n < 4 * FT else (up, n - 4 * FT)
                act.wait_ge(fg_full, n + 1)
                nc.scalar.activation(dst[:, m // 4, m % 4 * CHUNK:(m % 4 + 1) * CHUNK], quad[n % 4], ACT.Copy)\
                   .then_inc(fg_free, 1)

            for n in range(4 * FT + 4):
                if n == 4 * FT:
                    nc.scalar.activation(sd[:, 0:1], epst[:, :], ACT.Sigmoid).then_inc(table_in, 1)
                take_product(n)
            act.wait_ge(gm_ready, 2)
            for it in range(FT):
                if it:
                    for c in range(4):
                        take_product(4 * FT + 4 * it + c)
                    if it >= FT - N_DN:
                        dst, w = weights_to(N_WT + it - (FT - N_DN))
                        act.wait_ge(wd_full, it - (FT - N_DN) + 1)
                        nc.scalar.activation(dst, desk[:, 0:w], ACT.Copy).then_inc(wd_free, 1)
                if it >= 2:
                    act.wait_ge(gs_ready, it - 1)
                if it:
                    nc.scalar.activation(int_a[it % 2], gate[:, it, :], ACT.Copy, scale=scb[:, GATE, 1:2])\
                       .then_inc(g_int, 1)
                    act.wait_ge(g_int, it)
                else:
                    act.wait_ge(g0_int, 1)
                nc.scalar.activation(sig[it % 2], int_a[it % 2], ACT.Sigmoid,
                                     scale=scb[:, GATE, 0:1]).then_inc(sg_ready, 1)
            act.wait_ge(gm_ready, 3)
            for it in range(FT):
                if it - 2 in POOL_TILES:
                    act.wait_ge(o_pool, 3 * POOL_TILES.index(it - 2) + 2)
                elif it >= 2:
                    act.wait_ge(o_made, DVE_TILES.index(it - 2) + 1)
                if it not in DVE_UP:
                    nc.scalar.activation(int_a[it % 2], up[:, it, :], ACT.Copy, scale=scb[:, UP, 1:2])\
                      .then_inc(ug_int, 1)
                nc.scalar.activation(int_b[it % 2], gate[:, it, :], ACT.Copy, scale=scb[:, GS, 1:2]).then_inc(ug_int, 1)
            act.wait_ge(gm_ready, 4)
            for it in ACT_ROUNDS:
                nc.scalar.activation(gate[:, it, :], gate[:, it, :], ACT.Copy, bias=ROUND,
                                     scale=scb[:, OUT, 1:2]).then_inc(o_rnd, 1)

        @block.vector
        def _(dve):
            def layernorm_stats(tiles, base):
                for j in tiles:
                    if base == 0 and j % 4 == 0:
                        dve.wait_ge(x_in[j // 4], 16)
                    nc.vector.bn_stats(st[:, j, :], xacc[:, j, :]).then_inc(ln_stats, 1)
                for j in tiles:
                    dve.wait_ge(ln_stats, base + j + 1)
                    nc.vector.bn_aggr(mv[:, j, :], st[:, j, :]).then_inc(stats, 1)

            def take_turned(n, dst, cols, extra=None):
                dve.wait_ge(turned, n + 1)
                last = nc.vector.tensor_copy(dst, quad[n % 4][:, 0:cols])
                if extra is not None:
                    last = nc.vector.tensor_copy(extra, quad[n % 4][:, cols - 1:cols])
                last.then_inc(took_dve, 1)

            for n in range(1, 8, 2):
                take_turned(n, *turned_to(n))
            layernorm_stats(range(TOK), 0)
            dve.wait_ge(sd_ready, 1)
            nc.vector.reciprocal(rs[:, :], sd[:, :]).then_inc(rs_ready, 1)
            dve.wait_ge(rs_ready, 1)
            for j in range(TOK):
                nc.vector.tensor_scalar(xn[:, j, :], xacc[:, j, :], mv[:, j, 0:1], rs[:, j:j + 1],
                                        ALU.subtract, ALU.mult).then_inc(xn_ready, 1)
                if j == 7:
                    take_turned(9, *turned_to(9))

            for n in range(10, 16):
                take_turned(n, *turned_to(n))

            def unit_max(g, n, deep):
                bank = mring[(g * UNITS + n) % 6] if deep else mring[n % 2]
                h, j, u = n // (UNITS // 2), n % (UNITS // 2) // 4, n % 4
                if n == 0 and not (isinstance(g, int) and g == 0):
                    dve.wait_ge(nm_ready, g)
                dve.wait_ge(max_full, g * UNITS + (n + 1))
                nc.vector.tensor_reduce(mx[:, h, j, u:u + 1], bank[:, 0:MPIECES[u][1]], AX.X, ALU.max)\
                  .then_inc(max_free, 1)
                if n == UNITS - 1:
                    dve.wait_ge(max_free, g * UNITS + UNITS)
                    nc.vector.tensor_reduce(nm[:, :], mx[:, :, :, :].rearrange("p h j u -> p (h j) u"), AX.X,
                                            ALU.max, negate=True).then_inc(nm_ready, 1)

            def add(p, i):
                t, rows = i % TT, key_tile(i % TT)
                if t == 0:
                    return
                acc = psum_p[0:rows, 0:SPLIT]
                dve.wait_ge(exp_done, p * STEPS + (i + 1))
                if t == 1:
                    if not (isinstance(p, int) and p == 0 and i < TT):
                        dve.wait_ge(desk_full, desk_before(p, "D3'" if i < TT else f"D{i // TT - 1}") + 1)
                    nc.vector.tensor_tensor(acc, ring[:, (i - 1) % RING, 0:SPLIT], ring[:, i % RING, 0:SPLIT],
                                            ALU.add).then_inc(add_a, 2)
                else:
                    dve.wait_ge(add_a, p * STEPS + i)
                    nc.vector.tensor_tensor(acc, acc, ring[0:rows, i % RING, 0:SPLIT], ALU.add)\
                      .then_inc(add_a, 1)

            def desk_piece(p, name, b):
                k = name[0]
                if k == "O":
                    c, u = int(name[2]), "ab".index(name[1])
                    dve.wait_ge(desk_full, desk_before(p, name) + 1)
                    dst = xacc[:, 4 * c + 2 * u:4 * c + 2 * u + 2, :]
                    nc.vector.scalar_tensor_tensor(out=dst, in0=desk[:, :].rearrange("p (a m) -> p a m", m=M),
                                                   scalar=tg[:, 0:1], in1=dst, op0=ALU.mult, op1=ALU.add)\
                      .then_inc(desk_free, 1)
                if k == "W":
                    n = int(name[1:])
                    hi, w = weights_to(n)
                    lo = w_lo[:, n // 4, n % 4 // 2, 3 * P * (n % 2):3 * P * (n % 2 + 1)]
                    dve.wait_ge(w_split, n + 1)
                    nc.vector.tensor_tensor(lo, desk[:, 0:w], hi.bitcast(F32), ALU.subtract).then_inc(desk_free, 1)

            def normalise(done, q, p, name):
                cols = slice(q * P, (q + 1) * P)
                half = name[1]
                if q == 0:
                    dve.wait_ge(desk_free, desk_before(p, name) + 1)
                    dve.wait_ge(o_copied, done + 1)
                nc.vector.reciprocal(rden[:, cols], rden[:, cols]).then_inc(den_inv, 1)
                dve.wait_ge(den_inv, done * 4 + (q + 1))
                o = o_sb[:, int(half) % 2, cols]
                nc.vector.tensor_tensor(o, o, rden[:, cols], ALU.mult).then_inc(o_ready, 1)

            def quantise_weights(step):
                n, k, half = step // W_STEPS, step % W_STEPS // 2, step % 2
                each = FT * M // BLOCK // 2
                blocks = slice((2 * n + half) * each, (2 * n + half + 1) * each)
                first = half * FT // 2 + (n * FT if n < 2 else 0)
                wb = (w_nat if n < 2 else wd_nat)[:, first:first + FT // 2, :].rearrange("p a (k i) -> p (a k) i", i=BLOCK)
                if k == 0:
                    dve.wait_ge(wf_in[n], 16)
                    op = nc.vector.tensor_reduce(wmax[:, blocks], wb, AX.X, ALU.max, apply_absolute_value=True)
                else:
                    dve.wait_ge(w_step, step - 1)
                if k == 1:
                    op = nc.vector.tensor_scalar(wsc[:, blocks], wmax[:, blocks], 1.0 / WMAX, TINY, ALU.mult, ALU.max)
                if k == 2:
                    op = nc.vector.reciprocal(winv[:, blocks], wsc[:, blocks])
                if k == 3:
                    op = nc.vector.tensor_tensor(wb, wb, winv[:, blocks].unsqueeze(2).broadcast_to([P, each, BLOCK]),
                                                 ALU.mult)
                if k == 4:
                    op = nc.vector.tensor_scalar(wb, wb, ROUND, ROUND, ALU.add, ALU.subtract)
                if k == 5:
                    op = nc.vector.tensor_tensor(wb, wb, wsc[:, blocks].unsqueeze(2).broadcast_to([P, each, BLOCK]),
                                                 ALU.mult)
                op.then_inc(w_step, 1)

            def second_layernorm(tiles, p, name):
                dve.wait_ge(desk_free, desk_before(p, name) + 1)
                layernorm_stats(tiles, TOK)
                tiles = slice(tiles[0], tiles[-1] + 1)
                nc.vector.tensor_reduce(hi_x[:, tiles], xacc[:, tiles, :], AX.X, ALU.max).then_inc(x_range, 1)
                nc.vector.tensor_reduce(lo_x[:, tiles], xacc[:, tiles, :], AX.X, ALU.min).then_inc(x_range, 1)

            for n in range(UNITS):
                unit_max(0, n, True)
            for n in range(EARLY):
                unit_max(1, n, True)

            def window(p, b, first=False, last=False):
                for i in range(STEPS):
                    c, t = i // TT, i % TT
                    units, chunk = units_at(i, last)
                    for n in units[:AHEAD[2]]:
                        unit_max(p * CHUNKS + chunk, n, False)
                    if i:
                        add(p, i - 1)
                    if t in QUARTERS and not (first and c == 0):
                        normalise(p * CHUNKS + (c - 1), QUARTERS[t], p, "D3'" if c == 0 else f"D{c - 1}")
                    for n in units[AHEAD[2]:]:
                        unit_max(p * CHUNKS + chunk, n, False)
                    name = desk_order(first, last).get(i)
                    if name:
                        desk_piece(p, name, 1 - b)
                    if last and i in WEIGHTS_AT:
                        quantise_weights(WEIGHTS_AT.index(i))
                    if last and i in LAYERNORM_AT:
                        half = LAYERNORM_AT.index(i)
                        second_layernorm(range(2 * half, 2 * half + 2), p, f"Ob{half // 2}")
                add(p, STEPS - 1)

            dve.wait_ge(tg_ready, 1)
            window(0, 0, first=True)
            with dve.Fori(0, PAIRS // 2 - 1) as n:
                window(1 + 2 * n, 1)
                window(2 + 2 * n, 0)
            window(PAIRS - 1, 1, last=True)
            for q in range(4):
                normalise(PAIRS * CHUNKS - 1, q, PAIRS, "D3'")
            for name in OUT3:
                desk_piece(PAIRS, name, 0)
                if name[0] == "O":
                    first_tile = TOK - 4 + 2 * "ab".index(name[1])
                    second_layernorm(range(first_tile, first_tile + 2), PAIRS, name)


            def lane_maxima(n, it, src):
                nc.vector.tensor_reduce(lanes[:, n, it:it + 1], src, AX.X, ALU.max,
                                        apply_absolute_value=True).then_inc(lane_max, 1)

            def global_scales(k, n, m):
                dve.wait_ge(gm_row, k + 1)
                nc.vector.tensor_reduce(big[:, n:m], mb[0:1, 0:(m - n) * P].rearrange("a (t p) -> a t p", p=P),
                                        AX.X, ALU.max).then_inc(gm_step, 1)
                dve.wait_ge(gm_step, 5 * k + 1)
                dve.wait_ge(gm_unit, k)
                nc.vector.scalar_tensor_tensor(out=raw[:, n:m], in0=big[:, n:m], scalar=1.0 / QMAX,
                                               in1=unit[:, n:m], op0=ALU.mult, op1=ALU.mult).then_inc(gm_step, 1)
                dve.wait_ge(gm_step, 5 * k + 2)
                nc.vector.tensor_scalar(sc1[:, n:m, 0], raw[:, n:m], TINY, None, ALU.max).then_inc(gm_step, 1)
                dve.wait_ge(gm_step, 5 * k + 3)
                nc.vector.reciprocal(inv[:, n:m], sc1[:, n:m, 0]).then_inc(gm_step, 1)
                dve.wait_ge(gm_step, 5 * k + 4)
                nc.vector.tensor_tensor(sc1[:, n:m, 1], inv[:, n:m], unit[:, n:m], ALU.mult).then_inc(gm_step, 1)
                dve.wait_ge(gm_bc, k + 1)
                nc.vector.tensor_copy(scb[:, n:m, :], mb[:, CHUNK:CHUNK + 2 * (m - n)].rearrange(
                    "p (t a) -> p t a", a=2)).then_inc(gm_ready, 1)
                dve.wait_ge(gm_ready, k + 1)

            def largest(n, m, count, tiles):
                dve.wait_ge(lane_max, count)
                nc.vector.tensor_reduce(part[:, n:m], lanes[:, n:m, 0:tiles], AX.X, ALU.max).then_inc(gm_part, 1)

            dve.wait_ge(sd_ready, 2)
            nc.vector.reciprocal(rs[:, :], sd[:, :]).then_inc(rs_ready, 1)
            dve.wait_ge(x_range, 16)
            nc.vector.tensor_tensor(hi_x[:, :], hi_x[:, :], mv[:, :, 0], ALU.subtract).then_inc(x_dev, 1)
            nc.vector.tensor_tensor(lo_x[:, :], mv[:, :, 0], lo_x[:, :], ALU.subtract).then_inc(x_dev, 1)
            dve.wait_ge(x_dev, 2)
            nc.vector.tensor_tensor(hi_x[:, :], hi_x[:, :], lo_x[:, :], ALU.max).then_inc(x_dev, 1)
            dve.wait_ge(x_dev, 3)
            dve.wait_ge(rs_ready, 2)
            nc.vector.tensor_tensor(hi_x[:, :], hi_x[:, :], rs[:, :], ALU.mult).then_inc(x_dev, 1)
            dve.wait_ge(x_dev, 4)
            nc.vector.tensor_reduce(part[:, X:X + 1], hi_x[:, :], AX.X, ALU.max).then_inc(gm_part, 1)
            global_scales(0, X, X + 1)
            nc.vector.tensor_scalar(rsi[:, :], rs[:, :], scb[:, X, 1:2], None, ALU.mult).then_inc(x_dev, 1)
            dve.wait_ge(x_dev, 5)
            for c in range(4):
                for j in range(4 * c, 4 * c + 4):
                    nc.vector.tensor_scalar(xn2[:, j, :], xacc[:, j, :], mv[:, j, 0:1], rsi[:, j:j + 1],
                                            ALU.subtract, ALU.mult).then_inc(x_cen, 1)
            nc.vector.tensor_copy(unit[:, GATE:GATE + 1], sc1[:, X, 0:1]).then_inc(gm_unit, 1)
            for n in range(16, N_TURNED):
                hi, cols = turned_to(n)
                lo = xq_lo[:, n % 2, n % 8 // 2 * CHUNK:(n % 8 // 2 + 1) * CHUNK]
                dve.wait_ge(x_split, n - 15)
                nc.vector.scalar_tensor_tensor(out=lo, in0=quad[n % 4], scalar=ROUND, in1=hi.bitcast(F32),
                                               op0=ALU.subtract, op1=ALU.subtract).then_inc(took_dve, 1)

            for it in range(FT):
                quantise_weights(2 * W_STEPS + 2 * it)
                quantise_weights(2 * W_STEPS + 2 * it + 1)
                dve.wait_ge(fg_free, 4 * (it + 1))
                lane_maxima(GATE, it, gate[:, it, :])
            largest(GATE, GATE + 1, FT, FT)
            global_scales(1, GATE, GATE + 1)
            nc.vector.tensor_scalar(int_a[0], gate[:, 0, :], scb[:, GATE, 1:2], None, ALU.mult).then_inc(g0_int, 1)
            dve.wait_ge(g0_int, 1)
            for it in range(FT):
                dve.wait_ge(fg_free, 4 * FT + 4 * (it + 1))
                lane_maxima(UP, it, up[:, it, :])
                dve.wait_ge(s_int, it + 1)
                nc.vector.scalar_tensor_tensor(out=gate[:, it, :], in0=int_s[it % 2], scalar=SIG - 1,
                                               in1=int_a[it % 2], op0=ALU.min, op1=ALU.mult).then_inc(gs_ready, 1)
                dve.wait_ge(gs_ready, it + 1)
                lane_maxima(GS, it, gate[:, it, :])
            largest(UP, GS + 1, 3 * FT, FT)
            nc.vector.tensor_copy(unit[:, UP:UP + 1], sc1[:, X, 0:1])
            nc.vector.tensor_scalar(unit[:, GS:GS + 1], sc1[:, GATE, 0:1], 1.0 / SIG, None, ALU.mult)\
              .then_inc(gm_unit, 1)
            global_scales(2, UP, GS + 1)
            for n, it in enumerate(DVE_TILES):
                g = gate[:, it, :]
                if it in DVE_UP:
                    nc.vector.tensor_scalar(int_a[it % 2], up[:, it, :], scb[:, UP, 1:2], None, ALU.mult)\
                      .then_inc(u_int, 1)
                    dve.wait_ge(u_int, DVE_UP.index(it) + 1)
                dve.wait_ge(ug_int, ug_made(it))
                nc.vector.tensor_tensor(g, int_a[it % 2], int_b[it % 2], ALU.mult).then_inc(o_made, 1)
                dve.wait_ge(o_made, n + 1)
                lane_maxima(OUT, it, g)
                if n >= 2 and n - 2 < len(POOL_TILES):
                    dve.wait_ge(o_pool, 3 * (n - 1))
                    lane_maxima(OUT, POOL_TILES[n - 2], gate[:, POOL_TILES[n - 2], :])
            largest(OUT, OUT + 1, 4 * FT, FT)
            nc.vector.tensor_tensor(unit[:, OUT:OUT + 1], sc1[:, UP, 0:1], sc1[:, GS, 0:1], ALU.mult)\
              .then_inc(gm_unit, 1)
            global_scales(3, OUT, OUT + 1)
            nc.vector.tensor_scalar(tgs[:, :], tg[:, 1:2], scb[:, OUT, 0:1], None, ALU.mult).then_inc(gm_unit, 1)
            for it in range(FT):
                g = gate[:, it, :]
                if it in ACT_ROUNDS:
                    dve.wait_ge(o_rnd, ACT_ROUNDS.index(it) + 1)
                else:
                    nc.vector.tensor_scalar(g, g, scb[:, OUT, 1:2], ROUND, ALU.mult, ALU.add).then_inc(o_rnd2, 1)
                    dve.wait_ge(o_rnd2, it + 1 - sum(1 for t in ACT_ROUNDS if t < it))
                nc.vector.tensor_scalar(g, g, ROUND, None, ALU.subtract).then_inc(o_quant, 1)
            dve.wait_ge(gm_unit, 4)
            for j in range(TOK):
                dve.wait_ge(dn_full, j + 1)
                nc.vector.scalar_tensor_tensor(out=xacc[:, j, :], in0=result(j), scalar=tgs[:, :],
                                               in1=xacc[:, j, :], op0=ALU.mult, op1=ALU.add).then_inc(dn_free, 1)

        @block.tensor
        def _(pe):
            def mm(out_, lhsT, rhs, start=True, stop=True):
                return nc.tensor.matmul(out_, lhsT, rhs, start=start, stop=stop)

            def copied_out(n):
                if n in ACT_TURNED:
                    pe.wait_ge(took_act, ACT_TURNED.index(n) + 1)
                else:
                    pe.wait_ge(took_dve, DVE_TURNED.index(n) + 1)

            def turn(n):
                src, ready, value = turned_from(n)
                pe.wait_ge(ready, value)
                if n >= 4:
                    copied_out(n - 4)
                at = 0
                for ap, rows in src:
                    last = nc.tensor.transpose(quad[n % 4][:, at:at + rows], ap, ident[0:rows, 0:rows])
                    at += rows
                last.then_inc(turned, 1)

            def desk_piece(p, name, b):
                k = name[0]
                n = int(name[1:].rstrip("'+")) if k in "QKVTDW" else 0
                bank = prologue_bank(name) if isinstance(p, int) and p == -1 else desk
                if k in "QKV":
                    q, _ = prepared(p, name, b)
                    if n == 0:
                        pe.wait_ge({"Q": wq_in, "K": wk_in, "V": wv_in}[k], q * 32 + 32)
                if k == "W":
                    src, value = weights_from(n)
                    pe.wait_ge(w_step, value)
                if k == "D":
                    done = p * STEPS + (0 if name.endswith("'") else TT * (n + 1))
                    pe.wait_ge(add_a, done)
                    pe.wait_ge(add_b, done)
                if k == "O":
                    n = int(name[2])
                    prev = name.endswith("'")
                    pe.wait_ge(o_ready, (p - 1 if prev else p) * (4 * CHUNKS) + (4 * n + 2 + 2 * "ab".index(name[1])))
                    if not prev:
                        pe.wait_ge(wo_in, p * 16 + 16)
                if k == "T":
                    pe.wait_ge(nm_ready, p * CHUNKS + ((n or CHUNKS) + 1))
                if k == "W":
                    pe.wait_ge(desk_free, desk_before(p, name))
                    for j, ap in enumerate(src):
                        last = nc.tensor.transpose(desk[:, j * P:(j + 1) * P], ap, ident[:, :])
                elif not (isinstance(p, int) and p == -1):
                    pe.wait_ge(desk_free, desk_before(p, name))
                elif desk_before(p, name) >= 2:
                    pe.wait_ge(desk_free, desk_before(p, name) - 1)
                if k in "QK":
                    src, w = (xnT, w_qkv[0]) if k == "Q" else (ctxT, w_qkv[1])
                    c0, cols = (n * CHUNK, CHUNK) if k == "Q" else k_cols(n)
                    for kt in range(KT):
                        last = mm(bank[:, 0:cols], w[:, kt, :], src[:, kt, c0:c0 + cols], kt == 0, kt == KT - 1)
                if k == "V":
                    for t in range(4 * n, min(4 * n + 4, TT)):
                        rows = key_tile(t)
                        for kt in range(KT):
                            last = mm(bank[0:rows, (t % 4) * P:(t % 4 + 1) * P], ctxT[:, kt, t * P:t * P + rows],
                                      w_qkv[2][:, kt, :], kt == 0, kt == KT - 1)
                if k == "T":
                    last = nc.tensor.transpose(bank[0:2 * TOK // CHUNKS, 0:P], nm[:, :], ident[:, :])
                if k == "D":
                    for h in range(2):
                        last = mm(desk[h * D:(h + 1) * D, :], ones[:, :], psum_p[:, h * CHUNK:(h + 1) * CHUNK])
                if k == "O":
                    for j in range(2):
                        tok = (2 * "ab".index(name[1]) + j) * P
                        last = mm(desk[:, j * M:(j + 1) * M], o_sb[:, n % 2, tok:tok + P], w_o[:, :])
                last.then_inc(desk_full, 1)

            def unit_scores(q, c, n, b, deep):
                bank = mring[(c * UNITS + n) % 6] if deep else mring[n % 2]
                h, j, u = n // (UNITS // 2), c * 4 + n % (UNITS // 2) // 4, n % 4
                if n % (UNITS // 2) == 0:
                    pe.wait_ge(lo_ready, q * 16 + (2 * (len(BEFORE_M) + c) - (n == 0)))
                if deep and c * UNITS + n >= 6:
                    pe.wait_ge(max_free, c * UNITS + n - 5)
                if not deep:
                    pe.wait_ge(max_free, q * (CHUNKS * UNITS) + (c * UNITS + n - 1))
                k0, w = MPIECES[u]
                mm(bank[:, 0:w], q_hl[b][h][:, j * P:(j + 1) * P], k_hh[b][h][:, k0:k0 + w])\
                    .then_inc(max_full, 1)

            def scores(p, i, b, between):
                c, t = i // TT, i % TT
                rows = key_tile(t)
                if t == 0:
                    pe.wait_ge(shift_in, p * (32 * CHUNKS) + 32 * (c + 1))
                if isinstance(p, int) and p == 0 and i < 2:
                    pe.wait_ge(max_free, UNITS + EARLY)
                else:
                    pe.wait_ge(exp_done, p * STEPS + (i - 1))
                qs = slice(c * CHUNK, (c + 1) * CHUNK)
                for h in range(2):
                    dst = sc[i % 2][0:rows, h * CHUNK:(h + 1) * CHUNK]
                    deep = D + 1 if h == 0 else P
                    mm(dst, k_hh[b][h][:, t * P:t * P + rows], q_hl[b][h][:, qs], True, False)
                    last = mm(dst, k_l1[b][h][0:deep, t * P:t * P + rows], q_hm[b][h][0:deep, qs], False, True)
                    if h == 0:
                        between()
                last.then_inc(sc_full, 1)

            def values(p, i, b):
                c, t = i // TT, i % TT
                rows = key_tile(t)
                pe.wait_ge(exp_done, p * STEPS + (i + 1))
                if isinstance(p, int) and p == 0 and i == 0:
                    pe.wait_ge(desk_free, len(PROLOGUE))
                elif t == 0:
                    pe.wait_ge(o_copied, p * CHUNKS + c)
                for h in range(2):
                    last = mm(ob[h * D:(h + 1) * D, :], v_pair[b][0:rows, t, h * D:(h + 1) * D],
                              ring[0:rows, i % RING, h * CHUNK:(h + 1) * CHUNK], t == 0, t == TT - 1)
                last.then_inc(pv_done, 1)

            def window(p, b, first=False, last=False):
                for i in range(STEPS):
                    units, chunk = units_at(i, last)
                    ahead = (p, chunk) if chunk < CHUNKS else (p + 1, chunk - CHUNKS)
                    ub = b if chunk < CHUNKS else 1 - b

                    def between():
                        for n in units[:1]:
                            unit_scores(*ahead, n, ub, False)

                    scores(p, i, b, between)
                    for n in units[1:AHEAD[0]]:
                        unit_scores(*ahead, n, ub, False)
                    name = desk_order(first, last).get(i)
                    if name:
                        desk_piece(p, name, 1 - b)
                    for n in units[AHEAD[0]:AHEAD[1]]:
                        unit_scores(*ahead, n, ub, False)
                    if i:
                        values(p, i - 1, b)
                    for n in units[AHEAD[1]:]:
                        unit_scores(*ahead, n, ub, False)
                values(p, STEPS - 1, b)

            pe.wait_ge(consts, 1)
            for n in range(8):
                turn(n)
            for c, name in enumerate(BEFORE_M[:-1]):
                copied_out(4 + c)
                desk_piece(-1, name, 0)
            turn(8)
            turn(9)
            copied_out(8)
            copied_out(9)
            desk_piece(-1, BEFORE_M[-1], 0)
            for n in range(10, 16):
                turn(n)
            copied_out(15)
            for n in range(UNITS):
                unit_scores(0, 0, n, 0, True)
                if n in WITHIN_M:
                    desk_piece(-1, WITHIN_M[n], 0)
            for n in range(EARLY):
                unit_scores(0, 1, n, 0, True)
            desk_piece(-1, "T0", 0)
            pe.wait_ge(zeroed, 8)
            window(0, 0, first=True)
            with pe.Fori(0, PAIRS // 2 - 1) as n:
                window(1 + 2 * n, 1)
                window(2 + 2 * n, 0)
            window(PAIRS - 1, 1, last=True)
            for name in OUT3:
                desk_piece(PAIRS, name, 0)

            def find_scales(k, n, m):
                pe.wait_ge(gm_part, k + 1)
                for t in range(n, m):
                    last = mm(mb[0:1, (t - n) * P:(t - n + 1) * P], part[:, t:t + 1], ident[:, :])
                last.then_inc(gm_row, 1)
                pe.wait_ge(gm_step, 5 * k + 5)
                mm(mb[:, CHUNK:CHUNK + 2 * (m - n)], ones1[0:1, :],
                   sc1[0:1, n:m, :].rearrange("a t c -> a (t c)")).then_inc(gm_bc, 1)

            find_scales(0, X, X + 1)
            for n in range(16, N_TURNED):
                turn(n)
            copied_out(N_TURNED - 2)
            copied_out(N_TURNED - 1)

            def product(n):
                m, it, c = n // (4 * FT), n % (4 * FT) // 4, n % 4
                if n >= 4:
                    pe.wait_ge(fg_free, n - 3)
                terms = [(w, x_, kt) for kt in range(KT) for w, x_ in ((w_hi, xq_hi), (w_lo, xq_hi), (w_hi, xq_lo))]
                for k, (w, x_, kt) in enumerate(terms):
                    last = mm(quad[n % 4], w[:, m, kt, it * P:(it + 1) * P],
                              x_[:, kt, c * CHUNK:(c + 1) * CHUNK], k == 0, k == len(terms) - 1)
                last.then_inc(fg_full, 1)

            for n in range(8 * FT):
                product(n)
                if n % 4 == 3 and n // 4 - FT >= FT - N_DN:
                    k = n // 4 - FT - (FT - N_DN)
                    src, value = weights_from(N_WT + k)
                    pe.wait_ge(w_step, value)
                    if k:
                        pe.wait_ge(wd_free, k)
                    for j, ap in enumerate(src):
                        last = nc.tensor.transpose(desk[:, j * P:(j + 1) * P], ap, ident[:, :])
                    last.then_inc(wd_full, 1)
                if n == 4 * FT + 2:
                    find_scales(1, GATE, GATE + 1)
            find_scales(2, UP, GS + 1)
            find_scales(3, OUT, OUT + 1)
            pe.wait_ge(fg_free, 8 * FT)
            pe.wait_ge(gm_ready, 4)
            pe.wait_ge(wd_free, N_DN)

            def down(j, it):
                last = mm(result(j), gate[:, it, j * P:(j + 1) * P], w_dn[:, it, :], it == 0, it == FT - 1)
                if it == FT - 1:
                    last.then_inc(dn_full, 1)

            for it in range(FT):
                pe.wait_ge(o_quant, it + 1)
                for j in range(TOK // 2):
                    down(j, it)
            for j in range(TOK // 2, TOK):
                pe.wait_ge(dn_free, j - TOK // 2 + 1)
                for it in range(FT):
                    down(j, it)


_INS = ["x", "ctx_1024", "g_xattn", "g_ffn", "L0_xattn_Wq", "L0_xattn_Wk", "L0_xattn_Wv", "L0_xattn_Wo",
        "L0_ffn_w_gate", "L0_ffn_w_up", "L0_ffn_w_down"]


def kernel(**inputs):
    import concourse.bacc as bacc
    from concourse.bass_utils import run_bass_kernel_spmd as run

    nc = bacc.Bacc("TRN2", target_bir_lowering=False, num_devices=1)
    arrays, args = {}, []
    for name in _INS:
        a = np.ascontiguousarray(inputs[name])
        arrays[f"in_{name}"] = a
        args.append(nc.dram_tensor(f"in_{name}", a.shape, mybir.dt.from_np(a.dtype), kind="ExternalInput").ap())
    args.append(nc.dram_tensor("out_0", (1, S, M), F32, kind="ExternalOutput").ap())
    gated_block(nc, *args)
    r = run(nc, [arrays], core_ids=[0])
    return r.results[0]["out_0"]
```
